# Optimizing a Trainium2 kernel written in Bass

```python
import numpy as np
import jax
import jax.numpy as jnp

def _softmax(x, axis=-1):
    return jax.nn.softmax(x, axis=axis)

def _gelu(x):
    return jax.nn.gelu(x, approximate=True)

def _silu(x):
    return jax.nn.silu(x)

def _sigmoid(x):
    return jax.nn.sigmoid(x)

def _layernorm(x, axis=-1, eps=1e-05):
    m = jnp.mean(x, axis=axis, keepdims=True)
    v = jnp.var(x, axis=axis, keepdims=True)
    return (x - m) / jnp.sqrt(v + eps)

def _scatter_add(tgt, idx, src, axis=0):
    return tgt.at[idx].add(src)

def _segment_sum(src, seg, n):
    return jax.ops.segment_sum(src, seg, n)
kernel_name = 'mk_adaln_ffn_d1_seqx_r8_29704f'

def setup_inputs(seed: int=0):
    np.random.seed(seed)
    _w = jnp.asarray

    def _rec_inputs():
        import jax
        import jax.numpy as jnp
        _rk = jax.random.key(seed)
        x = -0.000125 + 0.9999 * jax.random.normal(jax.random.fold_in(_rk, 1), (128, 32, 512), jnp.float32)
        _lenS = 32 - jax.random.randint(jax.random.fold_in(_rk, 7), (128,), 0, max(1, 32 // 4) + 1, jnp.int32)
        _lenS2 = 32 - jax.random.randint(jax.random.fold_in(_rk, 8), (128,), 0, max(1, 32 // 4) + 1, jnp.int32)
        cond_128 = 0.0061147 + 1.02565 * jax.random.normal(jax.random.fold_in(_rk, 11), (128, 128), jnp.float32)
        fside_S_0 = -0.022604 + 0.987366 * jax.random.normal(jax.random.fold_in(_rk, 12), (32,), jnp.float32)
        return (x, cond_128, fside_S_0)
    x, cond_128, fside_S_0 = _rec_inputs()

    def _L0_cond_setup():
        import jax, jax.numpy as jnp
        import numpy as np
        from jax import lax
        N, C_IN, L = (32, 32, 512)
        C_OUT, K, GROUPS = (32, 9, 4)
        C_DIM, PAD, STRIDE = (128, 4, 1)
        key = jax.random.key(seed)
        k1, k2, k3, k4, k5 = jax.random.split(key, 5)
        x = jax.random.normal(k1, (N, C_IN, L), dtype=jnp.float32)
        c = jax.random.normal(k2, (N, C_DIM), dtype=jnp.float32)
        weight = jax.random.normal(k3, (C_OUT, C_IN // GROUPS, K), dtype=jnp.float32)
        c_weight = jax.random.normal(k4, (C_OUT, C_DIM), dtype=jnp.float32)
        bias = jax.random.normal(k5, (C_OUT,), dtype=jnp.float32)
        return {'x': x, 'c': c, 'weight': weight, 'c_weight': c_weight, 'bias': bias}
    _L0_cond_all = _L0_cond_setup()
    _L0_cond_in = {k: v for k, v in _L0_cond_all.items() if k in ('weight', 'c_weight')}
    del _L0_cond_all

    def _L0_ffn_setup():
        import jax, jax.numpy as jnp
        import numpy as np
        SCALING = 32.0 / 16.0
        key = jax.random.key(seed)
        ks = jax.random.split(key, 7)
        B, T, D, O, R, E = (4, 256, 512, 512, 16, 8)
        x = jax.random.normal(ks[0], (B, T, D), dtype=jnp.float32)
        base_W = jax.random.normal(ks[1], (O, D), dtype=jnp.float32) * D ** (-0.5)
        base_b = jax.random.normal(ks[2], (O,), dtype=jnp.float32) * 0.01
        router_W = jax.random.normal(ks[3], (2 * E - 1, D), dtype=jnp.float32) * D ** (-0.5)
        router_b = jax.random.normal(ks[4], (2 * E - 1,), dtype=jnp.float32) * 0.01
        A = jax.random.normal(ks[5], (E, R, D), dtype=jnp.float32) * D ** (-0.5)
        Bm = jax.random.normal(ks[6], (E, O, R), dtype=jnp.float32) * R ** (-0.5)
        assigned_idx = 0
        others = [i for i in range(E) if i != assigned_idx]
        expert_map = jnp.array([assigned_idx] * E + others, dtype=jnp.int32)
        return {'x': x, 'base_W': base_W, 'base_b': base_b, 'router_W': router_W, 'router_b': router_b, 'A': A, 'B': Bm, 'expert_map': expert_map}
    _L0_ffn_all = _L0_ffn_setup()
    _L0_ffn_in = {k: v for k, v in _L0_ffn_all.items() if k in ('base_W', 'base_b', 'router_W', 'router_b', 'A', 'B', 'expert_map')}
    del _L0_ffn_all
    return {'x': x, 'cond_128': cond_128, 'fside_S_0': fside_S_0, 'L0_cond_weight': _L0_cond_in['weight'], 'L0_cond_c_weight': _L0_cond_in['c_weight'], 'L0_ffn_base_W': _L0_ffn_in['base_W'], 'L0_ffn_base_b': _L0_ffn_in['base_b'], 'L0_ffn_router_W': _L0_ffn_in['router_W'], 'L0_ffn_router_b': _L0_ffn_in['router_b'], 'L0_ffn_A': _L0_ffn_in['A'], 'L0_ffn_B': _L0_ffn_in['B'], 'L0_ffn_expert_map': _L0_ffn_in['expert_map']}

def reference(x, cond_128, fside_S_0, L0_cond_weight, L0_cond_c_weight, L0_ffn_base_W, L0_ffn_base_b, L0_ffn_router_W, L0_ffn_router_b, L0_ffn_A, L0_ffn_B, L0_ffn_expert_map):
    import jax
    import jax.numpy as jnp

    def _L0_cond_ref(x, c, weight, c_weight, bias):
        import jax, jax.numpy as jnp
        import numpy as np
        from jax import lax
        N, C_IN, L = (32, 32, 512)
        C_OUT, K, GROUPS = (32, 9, 4)
        C_DIM, PAD, STRIDE = (128, 4, 1)
        out = lax.conv_general_dilated(x, weight, window_strides=(STRIDE,), padding=[(PAD, PAD)], dimension_numbers=('NCH', 'OIH', 'NCH'), feature_group_count=GROUPS)
        ctx = jnp.einsum('nd,od->no', c, c_weight)
        out = out + ctx[:, :, None] + bias[None, :, None]
        return out

    def _L0_ffn_ref(x, base_W, base_b, router_W, router_b, A, B, expert_map):
        import jax, jax.numpy as jnp
        import numpy as np
        SCALING = 32.0 / 16.0
        E = A.shape[0]
        base_out = jnp.einsum('btd,od->bto', x, base_W) + base_b
        logits = jnp.einsum('btd,nd->btn', x, router_W) + router_b
        probs = jax.nn.softmax(logits, axis=-1)
        topk_p, topk_i = jax.lax.top_k(probs, E)
        mapped = expert_map[topk_i]
        onehot = (mapped[..., None] == jnp.arange(E)).astype(x.dtype)
        w = jnp.einsum('btk,btke->bte', topk_p, onehot)
        h = jnp.einsum('btd,erd->bter', x, A)
        lora = jnp.einsum('bter,eor->bto', h * w[..., None], B) * SCALING
        return base_out + lora
    x = x + _L0_ffn_ref(_L0_cond_ref(x, cond_128, L0_cond_weight, L0_cond_c_weight, fside_S_0), L0_ffn_base_W, L0_ffn_base_b, L0_ffn_router_W, L0_ffn_router_b, L0_ffn_A, L0_ffn_B, L0_ffn_expert_map)
    return x

_drawn_inputs = setup_inputs


def setup_inputs(seed=0):
    import zlib

    import numpy as np

    out = dict(_drawn_inputs(seed))
    spreads = {}
    factors = {'L0_ffn_base_b': 64.0, 'L0_ffn_router_b': 49.948}
    for name, (base, spread) in spreads.items():
        noise = np.random.default_rng([zlib.crc32(name.encode()), seed]).standard_normal(out[name].shape)
        drawn = base * np.exp(spread * noise) if base else spread * noise
        out[name] = jnp.asarray(drawn.astype(out[name].dtype))
    for name, factor in factors.items():
        out[name] = (out[name] * factor).astype(out[name].dtype)
    return out
```

```python
from contextlib import ExitStack

import concourse.bass as bass
from concourse import mybir

F32 = mybir.dt.float32
F32R = mybir.dt.float32r
I32 = mybir.dt.int32
ALU = mybir.AluOpType
ACT = mybir.ActivationFunctionType
AX_X = mybir.AxisListType.X

P = 128
N, C, L = 128, 32, 512
TAPS, GROUPS, PAD = 9, 4, 4
E, R = 8, 16
ROUTES = 2 * E - 1
TOP = E
LORA_SCALE = 32.0 / 16.0
LOWEST = -3.0e38

Q = P // C
TILES = N // Q
PH = P // C
M = L // PH
BLOCKS = 3
MP = M + 2
HL = E * R + ROUTES

XRING = 4
UNROLL = 4


def build(nc, x_blocks, x_rows, conv_w, cond_t, cond_w, conv_b, base_w, base_b, down_w, router_b,
          up_w, expert_map, out):
    ctx = ExitStack()
    with ctx:
        def sb(name, shape, dt=F32):
            return ctx.enter_context(nc.sbuf_tensor(name, shape, dt))

        def pb(name, shape):
            return ctx.enter_context(nc.psum_tensor(name, shape, F32))

        def sem(name):
            return ctx.enter_context(nc.semaphore(name))

        conv_sb = sb("conv_sb", [P, BLOCKS, PH * C])
        cond_t_sb = sb("cond_t_sb", [P, N])
        cond_w_sb = sb("cond_w_sb", [P, C])
        conv_b_sb = sb("conv_b_sb", [P, C])
        ctx_nc = sb("ctx_nc", [P, C])
        ctx_all = sb("ctx_all", [P, N * C])
        base_sb = sb("base_sb", [P, PH, L])
        base_hi = sb("base_hi", [P, PH, L], F32R)
        base_lo = sb("base_lo", [P, PH, L], F32R)
        base_b_sb = sb("base_b_sb", [P, L])
        down_sb = sb("down_sb", [P, PH, HL])
        router_b_sb = sb("router_b_sb", [P, ROUTES])
        up_sb = sb("up_sb", [P, L])
        up_hi = sb("up_hi", [P, L], F32R)
        up_lo = sb("up_lo", [P, L], F32R)
        map_i = sb("map_i", [P, ROUTES], I32)
        map_f = sb("map_f", [P, ROUTES])
        is_expert = sb("is_expert", [P, E, ROUTES])
        ident = sb("ident", [P, P])

        xb = [sb(f"xb{i}", [P, Q, MP]) for i in range(XRING)]
        xr = [sb(f"xr{i}", [P, L]) for i in range(XRING)]
        y = [sb(f"y{i}", [P, PH, Q, C]) for i in range(2)]
        y_hi = [sb(f"y_hi{i}", [P, PH, P], F32R) for i in range(2)]
        y_lo = [sb(f"y_lo{i}", [P, PH, P], F32R) for i in range(2)]
        logits = [sb(f"logits{i}", [P, ROUTES]) for i in range(2)]
        top = [sb(f"top{i}", [P, TOP]) for i in range(2)]
        shifted = [sb(f"shifted{i}", [P, ROUTES]) for i in range(2)]
        exps = [sb(f"exps{i}", [P, ROUTES]) for i in range(2)]
        total = [sb(f"total{i}", [P, 1]) for i in range(2)]
        inv = [sb(f"inv{i}", [P, 1]) for i in range(2)]
        rest = [sb(f"rest{i}", [P, ROUTES]) for i in range(2)]
        chosen = [sb(f"chosen{i}", [P, ROUTES]) for i in range(2)]
        weight = [sb(f"weight{i}", [P, ROUTES]) for i in range(2)]
        spread = [sb(f"spread{i}", [P, E, ROUTES]) for i in range(2)]
        expert_w = [sb(f"expert_w{i}", [P, E]) for i in range(2)]
        hw = [sb(f"hw{i}", [P, E * R]) for i in range(2)]
        hw_hi = [sb(f"hw_hi{i}", [P, P], F32R) for i in range(2)]
        hw_lo = [sb(f"hw_lo{i}", [P, P], F32R) for i in range(2)]

        conv_ps = [pb(f"conv_ps{i}", [P, Q, PH, C]) for i in range(2)]
        down_ps = [pb(f"down_ps{i}", [P, 512]) for i in range(2)]
        hwt_ps = [pb(f"hwt_ps{i}", [P, 512]) for i in range(2)]
        out_ps = [pb(f"out_ps{i}", [P, L]) for i in range(2)]
        ctx_ps = hwt_ps[0][:, 0:C]

        conv_w_in = sem("conv_w_in")
        cond_in = sem("cond_in")
        base_in = sem("base_in")
        down_in = sem("down_in")
        up_in = sem("up_in")
        base_b_in = sem("base_b_in")
        router_in = sem("router_in")
        ctx_summed = sem("ctx_summed")
        ctx_biased = sem("ctx_biased")
        ctx_stored = sem("ctx_stored")
        ctx_in = sem("ctx_in")
        base_hi_ready = sem("base_hi_ready")
        base_lo_ready = sem("base_lo_ready")
        up_hi_ready = sem("up_hi_ready")
        up_lo_ready = sem("up_lo_ready")
        map_ready = sem("map_ready")
        ident_zeroed = sem("ident_zeroed")
        ident_ready = sem("ident_ready")
        xb_in = [sem(f"xb_in{i}") for i in range(XRING)]
        xr_in = [sem(f"xr_in{i}") for i in range(XRING)]
        stored = [sem(f"stored{i}") for i in range(XRING)]
        conv_done = sem("conv_done")
        y_ready = sem("y_ready")
        y_hi_ready = sem("y_hi_ready")
        y_lo_ready = sem("y_lo_ready")
        down_done = sem("down_done")
        logits_ready = sem("logits_ready")
        top_ready = sem("top_ready")
        shifted_ready = sem("shifted_ready")
        exps_ready = sem("exps_ready")
        inv_ready = sem("inv_ready")
        rest_ready = sem("rest_ready")
        chosen_ready = sem("chosen_ready")
        weight_ready = sem("weight_ready")
        spread_ready = sem("spread_ready")
        expert_w_ready = sem("expert_w_ready")
        hw_ready = sem("hw_ready")
        hwt_done = sem("hwt_done")
        hw_hi_ready = sem("hw_hi_ready")
        hw_lo_ready = sem("hw_lo_ready")
        out_done = sem("out_done")
        xr_biased = sem("xr_biased")
        out_added = sem("out_added")

        ctx_dram = nc.dram_tensor("ctx_dram", (N, C), F32, kind="Internal").ap()

        def each_step(eng, step):
            for t in range(-1, UNROLL):
                step(t, t % UNROLL)
            with eng.Fori(1, TILES // UNROLL - 1) as group:
                for k in range(UNROLL):
                    step(group * UNROLL + k, k)
            for t in range(TILES - UNROLL, TILES):
                step(t, t % UNROLL)

        def from_tile(t, least):
            return not isinstance(t, int) or t >= least

        def up_to_tile(t, most):
            return not isinstance(t, int) or t <= most

        block = ctx.enter_context(nc.Block())

        @block.sync
        def _(sync):
            sync.dma_start(conv_sb[:, :, :], conv_w).then_inc(conv_w_in, 16)
            sync.dma_start(xb[0][:, :, :], x_blocks[0]).then_inc(xb_in[0], 16)
            sync.dma_start(down_sb[:, :, :], down_w).then_inc(down_in, 16)
            for h in range(2):
                rows = slice(h * PH // 2, (h + 1) * PH // 2)
                sync.dma_start(base_sb[:, rows, :], base_w[:, rows, :]).then_inc(base_in, 16)
            sync.dma_start(xb[1][:, :, :], x_blocks[1]).then_inc(xb_in[1], 16)
            sync.dma_start(up_sb[:, :], up_w).then_inc(up_in, 16)
            sync.dma_start(xr[0][:, :], x_rows[0]).then_inc(xr_in[0], 16)
            for t in range(2, XRING):
                sync.dma_start(xb[t][:, :, :], x_blocks[t]).then_inc(xb_in[t], 16)
            sync.dma_start(xr[1][:, :], x_rows[1]).then_inc(xr_in[1], 16)

            def step(t, k):
                if not from_tile(t, 0):
                    return
                if up_to_tile(t, TILES - 1 - XRING):
                    sync.wait_ge(conv_done, t + 1)
                    sync.dma_start(xb[k][:, :, :], x_blocks[t + XRING]).then_inc(xb_in[k], 16)
                if from_tile(t, 1):
                    sync.wait_ge(out_added, t)
                    sync.dma_start(out[t - 1], xr[(k - 1) % XRING][:, :])\
                        .then_inc(stored[(k - 1) % XRING], 16)
                if up_to_tile(t, TILES - 3):
                    if from_tile(t, 2):
                        sync.wait_ge(stored[(k - 2) % XRING], (t - 2 - (k - 2) % XRING) * 4 + 16)
                    sync.dma_start(xr[(k + 2) % XRING][:, :], x_rows[t + 2])\
                        .then_inc(xr_in[(k + 2) % XRING], 16)

            each_step(sync, step)
            sync.wait_ge(out_added, TILES)
            sync.dma_start(out[TILES - 1], xr[(TILES - 1) % XRING][:, :])\
                .then_inc(stored[(TILES - 1) % XRING], 16)
            for i in range(XRING):
                sync.wait_ge(stored[i], 16 * (TILES // XRING))

        @block.scalar
        def _(act):
            act.dma_start(cond_t_sb[:, :], cond_t).then_inc(cond_in, 16)
            act.dma_start(cond_w_sb[:, :], cond_w).then_inc(cond_in, 16)
            act.dma_start(conv_b_sb[:, :], conv_b.partition_broadcast(P)).then_inc(cond_in, 16)
            act.dma_start(router_b_sb[:, :], router_b.partition_broadcast(P)).then_inc(router_in, 16)
            act.dma_start(map_i[:, :], expert_map.partition_broadcast(P)).then_inc(router_in, 16)
            act.dma_start(base_b_sb[:, :], base_b.partition_broadcast(P)).then_inc(base_b_in, 16)
            act.wait_ge(ctx_biased, 1)
            act.dma_start(ctx_dram, ctx_nc[:, :]).then_inc(ctx_stored, 16)
            act.wait_ge(ctx_stored, 16)
            act.dma_start(ctx_all[:, :], ctx_dram.rearrange("n c -> (n c)").partition_broadcast(P))\
                .then_inc(ctx_in, 16)
            act.wait_ge(base_in, 32)
            for r in range(PH):
                nc.scalar.activation(base_hi[:, r, :], base_sb[:, r, :], ACT.Copy)\
                    .then_inc(base_hi_ready, 1)
            act.wait_ge(up_in, 16)
            nc.scalar.activation(up_hi[:, :], up_sb[:, :], ACT.Copy, scale=LORA_SCALE)\
                .then_inc(up_hi_ready, 1)

            def step(t, k):
                if from_tile(t, 0):
                    act.wait_ge(shifted_ready, t + 1)
                    nc.scalar.activation(exps[k % 2][:, :], shifted[k % 2][:, :], ACT.Exp,
                                         accum_out=total[k % 2][:, :]).then_inc(exps_ready, 1)
                if up_to_tile(t, TILES - 2):
                    act.wait_ge(y_ready, t + 2)
                    if from_tile(t, 1):
                        act.wait_ge(out_done, t)
                        act.wait_ge(y_lo_ready, t)
                    nc.scalar.activation(y_hi[(k + 1) % 2][:, :, :],
                                         y[(k + 1) % 2][:, :, :, :].rearrange("p r q c -> p r (q c)"),
                                         ACT.Copy).then_inc(y_hi_ready, 1)
                if from_tile(t, 0):
                    act.wait_ge(hwt_done, t + 1)
                    if from_tile(t, 2):
                        act.wait_ge(out_done, t - 1)
                    nc.scalar.activation(hw_hi[k % 2][:, :], hwt_ps[k % 2][:, 0:P], ACT.Copy)\
                        .then_inc(hw_hi_ready, 1)

            each_step(act, step)

        @block.gpsimd
        def _(pool):
            nc.gpsimd.memset(ident[:, :], 0.0).then_inc(ident_zeroed, 1)
            pool.wait_ge(ident_zeroed, 1)
            nc.gpsimd.affine_select(out=ident[:, :], in_=ident[:, :], compare_op=ALU.not_equal,
                                    fill=1.0, base=0, pattern=[[-1, P]], channel_multiplier=1)\
                .then_inc(ident_ready, 1)
            for r in range(PH):
                pool.wait_ge(base_hi_ready, r + 1)
                nc.gpsimd.tensor_tensor(base_lo[:, r, :], base_sb[:, r, :],
                                        base_hi[:, r, :].bitcast(F32), ALU.subtract)\
                    .then_inc(base_lo_ready, 1)
            pool.wait_ge(base_b_in, 16)

            def step(t, k):
                if up_to_tile(t, TILES - 2):
                    pool.wait_ge(y_hi_ready, t + 2)
                    nc.gpsimd.tensor_tensor(y_lo[(k + 1) % 2][:, :, :],
                                            y[(k + 1) % 2][:, :, :, :].rearrange("p r q c -> p r (q c)"),
                                            y_hi[(k + 1) % 2][:, :, :].bitcast(F32), ALU.subtract)\
                        .then_inc(y_lo_ready, 1)
                if from_tile(t, 0):
                    pool.wait_ge(xr_in[k], (t - k) * 4 + 16)
                    nc.gpsimd.tensor_tensor(xr[k][:, :], xr[k][:, :], base_b_sb[:, :], ALU.add)\
                        .then_inc(xr_biased, 1)

            each_step(pool, step)

        @block.tensor
        def _(pe):
            pe.wait_ge(cond_in, 48)
            nc.tensor.matmul(ctx_ps, cond_t_sb[:, :], cond_w_sb[:, :], start=True, stop=True)\
                .then_inc(ctx_summed, 1)
            pe.wait_ge(conv_w_in, 16)

            def conv(t, k):
                pe.wait_ge(xb_in[k], (t - k) * 4 + 16)
                if from_tile(t, 2):
                    pe.wait_ge(y_ready, t - 1)
                for q in range(Q):
                    for b in range(BLOCKS):
                        mm = nc.tensor.matmul(conv_ps[k % 2][:, q, :, :], xb[k][:, q, b:b + M],
                                              conv_sb[:, b, :], start=b == 0, stop=b == BLOCKS - 1)
                mm.then_inc(conv_done, 1)

            def down(t, k):
                pe.wait_ge(y_ready, t + 1)
                if from_tile(t, 2):
                    pe.wait_ge(hw_ready, t - 1)
                for r in range(PH):
                    mm = nc.tensor.matmul(down_ps[k % 2][:, 0:HL],
                                          y[k % 2][:, r, :, :].rearrange("p q c -> p (q c)"),
                                          down_sb[:, r, :], start=r == 0, stop=r == PH - 1)
                mm.then_inc(down_done, 1)

            def step(t, k):
                if up_to_tile(t, TILES - 2):
                    conv(t + 1, (k + 1) % UNROLL)
                if not from_tile(t, 0):
                    pe.wait_ge(down_in, 16)
                    down(t + 1, (k + 1) % UNROLL)
                    pe.wait_ge(base_lo_ready, PH)
                    return
                pe.wait_ge(y_lo_ready, t + 1)
                if from_tile(t, 2):
                    pe.wait_ge(out_added, t - 1)
                for r in range(PH):
                    for a, w in ((y_hi, base_hi), (y_hi, base_lo), (y_lo, base_hi)):
                        nc.tensor.matmul(out_ps[k % 2][:, :], a[k % 2][:, r, :], w[:, r, :],
                                         start=r == 0 and w is base_hi and a is y_hi, stop=False)
                pe.wait_ge(hw_ready, t + 1)
                if not from_tile(t, 1):
                    pe.wait_ge(ident_ready, 1)
                    pe.wait_ge(ctx_biased, 1)
                    pe.wait_ge(up_lo_ready, 1)
                if from_tile(t, 2):
                    pe.wait_ge(hw_lo_ready, t - 1)
                nc.tensor.transpose(hwt_ps[k % 2][:, 0:P], hw[k % 2][:, :], ident[:, :])\
                    .then_inc(hwt_done, 1)
                if up_to_tile(t, TILES - 2):
                    down(t + 1, (k + 1) % UNROLL)
                pe.wait_ge(hw_hi_ready, t + 1)
                nc.tensor.matmul(out_ps[k % 2][:, :], hw_hi[k % 2][:, :], up_hi[:, :],
                                 start=False, stop=False)
                nc.tensor.matmul(out_ps[k % 2][:, :], hw_hi[k % 2][:, :], up_lo[:, :],
                                 start=False, stop=False)
                pe.wait_ge(hw_lo_ready, t + 1)
                nc.tensor.matmul(out_ps[k % 2][:, :], hw_lo[k % 2][:, :], up_hi[:, :],
                                 start=False, stop=True).then_inc(out_done, 1)

            each_step(pe, step)

        @block.vector
        def _(dve):
            dve.wait_ge(cond_in, 48)
            dve.wait_ge(ctx_summed, 1)
            nc.vector.tensor_tensor(ctx_nc[:, :], ctx_ps, conv_b_sb[:, :], ALU.add)\
                .then_inc(ctx_biased, 1)
            dve.wait_ge(router_in, 32)
            nc.vector.tensor_copy(map_f[:, :], map_i[:, :]).then_inc(map_ready, 1)
            dve.wait_ge(map_ready, 1)
            for e in range(E):
                nc.vector.tensor_scalar(is_expert[:, e, :], map_f[:, :], float(e), None,
                                        ALU.is_equal).then_inc(map_ready, 1)
            dve.wait_ge(up_hi_ready, 1)
            nc.vector.scalar_tensor_tensor(out=up_lo[:, :], in0=up_sb[:, :], scalar=LORA_SCALE,
                                           in1=up_hi[:, :].bitcast(F32), op0=ALU.mult,
                                           op1=ALU.subtract).then_inc(up_lo_ready, 1)
            dve.wait_ge(map_ready, 1 + E)
            dve.wait_ge(ctx_in, 16)

            def add_out(t, k):
                dve.wait_ge(xr_biased, t + 1)
                dve.wait_ge(out_done, t + 1)
                nc.vector.tensor_tensor(xr[k][:, :], out_ps[k % 2][:, :], xr[k][:, :], ALU.add)\
                    .then_inc(out_added, 1)

            def add_router_b(t, k):
                dve.wait_ge(down_done, t + 1)
                nc.vector.tensor_tensor(logits[k % 2][:, :], down_ps[k % 2][:, E * R:HL],
                                        router_b_sb[:, :], ALU.add).then_inc(logits_ready, 1)

            def route(t, k):
                i = k % 2
                nc.vector.max(top[i][:, :], logits[i][:, :]).then_inc(top_ready, 1)
                dve.wait_ge(top_ready, t + 1)
                nc.vector.tensor_scalar(shifted[i][:, :], logits[i][:, :], top[i][:, 0:1], None,
                                        ALU.subtract).then_inc(shifted_ready, 1)
                nc.vector.match_replace(rest[i][:, :], top[i][:, :], logits[i][:, :], LOWEST)\
                    .then_inc(rest_ready, 1)
                dve.wait_ge(rest_ready, t + 1)
                nc.vector.tensor_tensor(chosen[i][:, :], rest[i][:, :], logits[i][:, :],
                                        ALU.not_equal).then_inc(chosen_ready, 1)
                dve.wait_ge(exps_ready, t + 1)
                nc.vector.reciprocal(inv[i][:, :], total[i][:, :]).then_inc(inv_ready, 1)
                dve.wait_ge(chosen_ready, t + 1)
                dve.wait_ge(inv_ready, t + 1)
                nc.vector.scalar_tensor_tensor(out=weight[i][:, :], in0=exps[i][:, :],
                                               scalar=inv[i][:, 0:1], in1=chosen[i][:, :],
                                               op0=ALU.mult, op1=ALU.mult).then_inc(weight_ready, 1)
                dve.wait_ge(weight_ready, t + 1)
                nc.vector.tensor_tensor(spread[i][:, :, :], is_expert[:, :, :],
                                        weight[i][:, :].unsqueeze(1).to_broadcast([P, E, ROUTES]),
                                        ALU.mult).then_inc(spread_ready, 1)
                dve.wait_ge(spread_ready, t + 1)
                nc.vector.tensor_reduce(expert_w[i][:, :], spread[i][:, :, :], AX_X, ALU.add)\
                    .then_inc(expert_w_ready, 1)
                dve.wait_ge(expert_w_ready, t + 1)
                if from_tile(t, 2):
                    dve.wait_ge(hwt_done, t - 1)
                nc.vector.tensor_tensor(
                    hw[i][:, :].rearrange("p (e r) -> p e r", e=E),
                    down_ps[i][:, 0:E * R].rearrange("p (e r) -> p e r", e=E),
                    expert_w[i][:, :].unsqueeze(2).to_broadcast([P, E, R]),
                    ALU.mult).then_inc(hw_ready, 1)

            def condition(t, k):
                i = k % 2
                dve.wait_ge(conv_done, t + 1)
                if from_tile(t, 2):
                    dve.wait_ge(down_done, t - 1)
                    dve.wait_ge(y_lo_ready, t - 1)
                c = ctx_all[:, bass.ds(t * (Q * C), Q * C)].rearrange("p (q c) -> p q c", q=Q)
                nc.vector.tensor_tensor(y[i][:, :, :, :].rearrange("p r q c -> p q r c"),
                                        conv_ps[i][:, :, :, :],
                                        c.unsqueeze(2).to_broadcast([P, Q, PH, C]),
                                        ALU.add).then_inc(y_ready, 1)

            def step(t, k):
                if from_tile(t, 0):
                    add_router_b(t, k)
                    dve.wait_ge(logits_ready, t + 1)
                if from_tile(t, 1):
                    add_out(t - 1, (k - 1) % UNROLL)
                if from_tile(t, 0):
                    route(t, k)
                if up_to_tile(t, TILES - 2):
                    condition(t + 1, (k + 1) % UNROLL)
                if from_tile(t, 0):
                    dve.wait_ge(hw_hi_ready, t + 1)
                    if from_tile(t, 2):
                        dve.wait_ge(out_done, t - 1)
                    nc.vector.tensor_tensor(hw_lo[k % 2][:, :], hwt_ps[k % 2][:, 0:P],
                                            hw_hi[k % 2][:, :].bitcast(F32), ALU.subtract)\
                        .then_inc(hw_lo_ready, 1)

            each_step(dve, step)
            add_out(TILES - 1, (TILES - 1) % UNROLL)


def kernel(x, cond_128, fside_S_0, L0_cond_weight, L0_cond_c_weight, L0_ffn_base_W, L0_ffn_base_b,
           L0_ffn_router_W, L0_ffn_router_b, L0_ffn_A, L0_ffn_B, L0_ffn_expert_map):
    import numpy as np
    from concourse import bacc
    from concourse.bass_utils import run_bass_kernel_spmd

    x = np.asarray(x)
    blocks = x.reshape(N, C, M, PH).transpose(3, 1, 0, 2)
    blocks = np.pad(blocks, ((0, 0), (0, 0), (0, 0), (1, 1))).reshape(P, TILES, Q, MP)

    w = np.asarray(L0_cond_weight)
    per = C // GROUPS
    conv = np.zeros((PH, C, BLOCKS, PH, C), w.dtype)
    for b in range(BLOCKS):
        for s in range(PH):
            for r in range(PH):
                tap = PH * b + s - r
                if 0 <= tap < TAPS:
                    for g in range(GROUPS):
                        own = slice(g * per, (g + 1) * per)
                        conv[s, own, b, r, own] = w[own, :, tap].T

    def by_position(a):
        a = np.asarray(a).reshape(-1, M, PH)
        return a.transpose(1, 2, 0)

    down = np.concatenate([by_position(L0_ffn_A), by_position(L0_ffn_router_W)], axis=2)
    given = {
        "x_blocks": blocks.transpose(1, 0, 2, 3),
        "x_rows": x.reshape(TILES, P, L),
        "conv_w": conv.reshape(P, BLOCKS, PH * C),
        "cond_t": np.asarray(cond_128).T,
        "cond_w": np.asarray(L0_cond_c_weight).T,
        "conv_b": fside_S_0,
        "base_w": by_position(L0_ffn_base_W),
        "base_b": L0_ffn_base_b,
        "down_w": down,
        "router_b": L0_ffn_router_b,
        "up_w": np.asarray(L0_ffn_B).transpose(0, 2, 1).reshape(E * R, L),
        "expert_map": L0_ffn_expert_map,
    }
    nc = bacc.Bacc("TRN2", target_bir_lowering=False, num_devices=1)
    arrays, args = {}, []
    for name, a in given.items():
        a = np.ascontiguousarray(a)
        arrays[name] = a
        args.append(nc.dram_tensor(name, a.shape, mybir.dt.from_np(a.dtype), kind="ExternalInput").ap())
    out = nc.dram_tensor("out", (TILES, P, L), F32, kind="ExternalOutput").ap()
    build(nc, *args, out)
    r = run_bass_kernel_spmd(nc, [arrays], core_ids=[0])
    return r.results[0]["out"].reshape(N, C, L)
```

```python
from contextlib import ExitStack

import concourse.bass as bass
from concourse import mybir

F32 = mybir.dt.float32
BF16 = mybir.dt.bfloat16
F32R = mybir.dt.float32r
I32 = mybir.dt.int32
ALU = mybir.AluOpType
ACT = mybir.ActivationFunctionType
AX_X = mybir.AxisListType.X

P = 128
N, C, L = 128, 32, 512
TAPS, GROUPS, PAD = 9, 4, 4
E, R = 8, 16
ROUTES = 2 * E - 1
TOP = E
LORA_SCALE = 32.0 / 16.0
LOWEST = -3.0e38

Q = P // C
TILES = N // Q
HALVES = 2
CH = C // HALVES
PAIR = 2 * Q
BP = P // CH
M = L // BP
MI = M + 1
BLOCKS = 2
RUNS = BP // 2
HL = E * R + ROUTES

XRING = 4
UNROLL = 4
WARM_UP = 10


def build(nc, x_blocks, x_rows, conv_w, cond, base_w, down_w, up_w, biases, expert_map, out):
    ctx = ExitStack()
    with ctx:
        def sb(name, shape, dt=F32):
            return ctx.enter_context(nc.sbuf_tensor(name, shape, dt))

        def pb(name, shape):
            return ctx.enter_context(nc.psum_tensor(name, shape, F32))

        def sem(name):
            return ctx.enter_context(nc.semaphore(name))

        conv_sb = sb("conv_sb", [P, HALVES, BLOCKS, P])
        conv_hi = sb("conv_hi", [P, HALVES, BLOCKS, P], F32R)
        conv_lo = sb("conv_lo", [P, HALVES, BLOCKS, P], F32R)
        cond_in_sb = sb("cond_in_sb", [P, N + HALVES * P + HALVES])
        cond_t_sb = cond_in_sb[:, 0:N]
        cond_w_sb = cond_in_sb[:, N:N + HALVES * P].rearrange("p (h q) -> p h q", h=HALVES)
        conv_b_sb = cond_in_sb[:, N + HALVES * P:]
        cond_sb = sb("cond_sb", [P, HALVES, N])
        base_sb = sb("base_sb", [P, RUNS, L])
        base_hi = sb("base_hi", [P, RUNS, L], F32R)
        base_lo = sb("base_lo", [P, RUNS, L], F32R)
        biases_sb = sb("biases_sb", [P, L + ROUTES])
        base_b_sb = biases_sb[:, 0:L]
        router_b_sb = biases_sb[:, L:]
        down_sb = sb("down_sb", [P, RUNS, HL])
        up_sb = sb("up_sb", [P, L])
        up_hi = sb("up_hi", [P, L], F32R)
        up_lo = sb("up_lo", [P, L], F32R)
        map_i = sb("map_i", [P, ROUTES], I32)
        map_f = sb("map_f", [P, ROUTES])
        is_expert = sb("is_expert", [P, E, ROUTES])
        ident = sb("ident", [P, P])
        zeros = sb("zeros", [P, L], BF16)
        zero_exp = sb("zero_exp", [P, 1])

        x_in = [sb(f"x_in{i}", [P, HALVES, PAIR, MI]) for i in range(2)]
        x_hi = [sb(f"x_hi{i}", [P, HALVES, PAIR, MI], F32R) for i in range(2)]
        x_lo = [sb(f"x_lo{i}", [P, HALVES, PAIR, MI], F32R) for i in range(2)]
        y_rows = [sb(f"y_rows{i}", [P, HALVES, PAIR, M]) for i in range(2)]
        xr = [sb(f"xr{i}", [P, L]) for i in range(XRING)]
        y = [sb(f"y{i}", [P, RUNS, P]) for i in range(2)]
        y_hi = [sb(f"y_hi{i}", [P, RUNS, P], F32R) for i in range(2)]
        y_lo = [sb(f"y_lo{i}", [P, RUNS, P], F32R) for i in range(2)]
        logits = [sb(f"logits{i}", [P, ROUTES]) for i in range(2)]
        best = [sb(f"best{i}", [P, 1]) for i in range(2)]
        top = [sb(f"top{i}", [P, TOP]) for i in range(2)]
        shifted = [sb(f"shifted{i}", [P, ROUTES]) for i in range(2)]
        exps = [sb(f"exps{i}", [P, ROUTES]) for i in range(2)]
        total = [sb(f"total{i}", [P, 1]) for i in range(2)]
        inv = [sb(f"inv{i}", [P, 1]) for i in range(2)]
        rest = [sb(f"rest{i}", [P, ROUTES]) for i in range(2)]
        chosen = [sb(f"chosen{i}", [P, ROUTES]) for i in range(2)]
        weight = [sb(f"weight{i}", [P, ROUTES]) for i in range(2)]
        spread = [sb(f"spread{i}", [P, E, ROUTES]) for i in range(2)]
        expert_w = [sb(f"expert_w{i}", [P, E]) for i in range(2)]
        hw = [sb(f"hw{i}", [P, E * R]) for i in range(2)]
        hw_hi = [sb(f"hw_hi{i}", [P, P], F32R) for i in range(2)]
        hw_lo = [sb(f"hw_lo{i}", [P, P], F32R) for i in range(2)]

        conv_ps = [pb(f"conv_ps{h}", [P, PAIR, M]) for h in range(HALVES)]
        turn_ps = pb("turn_ps", [P, Q // 2, HALVES, BP, CH])
        down_ps = [pb(f"down_ps{i}", [P, 512]) for i in range(2)]
        hwt_ps = pb("hwt_ps", [P, 512])
        out_ps = [pb(f"out_ps{i}", [P, L]) for i in range(2)]
        cond_ps = down_ps[1][:, 0:HALVES * N].rearrange("p (h n) -> p h n", h=HALVES)

        conv_w_in = sem("conv_w_in")
        cond_in = sem("cond_in")
        base_in = [sem(f"base_in{i}") for i in range(RUNS // 2)]
        down_in = sem("down_in")
        up_in = sem("up_in")
        biases_in = sem("biases_in")
        map_in = sem("map_in")
        zeros_ready = sem("zeros_ready")
        conv_hi_ready = sem("conv_hi_ready")
        conv_lo_ready = sem("conv_lo_ready")
        x_lo_first = sem("x_lo_first")
        cond_summed = sem("cond_summed")
        cond_biased = sem("cond_biased")
        base_hi_ready = sem("base_hi_ready")
        base_lo_ready = sem("base_lo_ready")
        up_hi_ready = sem("up_hi_ready")
        up_lo_ready = sem("up_lo_ready")
        map_ready = sem("map_ready")
        ident_zeroed = sem("ident_zeroed")
        ident_ready = sem("ident_ready")
        x_loaded = [sem(f"x_loaded{i}") for i in range(2)]
        xr_loaded = [sem(f"xr_loaded{i}") for i in range(XRING)]
        stored = [sem(f"stored{i}") for i in range(XRING)]
        x_hi_ready = sem("x_hi_ready")
        x_lo_ready = sem("x_lo_ready")
        conv_done = sem("conv_done")
        y_rows_ready = sem("y_rows_ready")
        turned = sem("turned")
        y_even_ready = sem("y_even_ready")
        y_odd_ready = sem("y_odd_ready")
        y_hi_ready = sem("y_hi_ready")
        y_lo_ready = sem("y_lo_ready")
        down_done = sem("down_done")
        logits_ready = sem("logits_ready")
        top_ready = sem("top_ready")
        best_ready = sem("best_ready")
        shifted_ready = sem("shifted_ready")
        exps_ready = sem("exps_ready")
        inv_ready = sem("inv_ready")
        rest_ready = sem("rest_ready")
        chosen_ready = sem("chosen_ready")
        weight_ready = sem("weight_ready")
        spread_ready = sem("spread_ready")
        expert_w_ready = sem("expert_w_ready")
        hw_ready = sem("hw_ready")
        hwt_done = sem("hwt_done")
        hw_hi_ready = sem("hw_hi_ready")
        hw_lo_ready = sem("hw_lo_ready")
        out_done = sem("out_done")
        xr_biased = sem("xr_biased")
        out_added = sem("out_added")

        def each_step(eng, step):
            for t in range(-2, UNROLL):
                step(t, t % UNROLL, t // 2)
            with eng.Fori(1, TILES // UNROLL - 2) as group:
                for k in range(UNROLL):
                    step(group * UNROLL + k, k, group * (UNROLL // 2) + k // 2)
            for t in range(TILES - 2 * UNROLL, TILES):
                step(t, t % UNROLL, t // 2)

        def from_tile(t, least):
            return not isinstance(t, int) or t >= least

        def up_to_tile(t, most):
            return not isinstance(t, int) or t <= most

        def copy_turned(copy, t, k, j, ready):
            for low in range(2):
                src = turn_ps[j * M:(j + 1) * M, :, :, low * RUNS:(low + 1) * RUNS, :]
                dst = y[k % 2][low * M:(low + 1) * M, :, j * (P // 2):(j + 1) * (P // 2)]
                copy(dst.rearrange("m r (a o) -> m a r o", o=CH),
                     src.rearrange("m a h r o -> m (a h) r o")).then_inc(ready, 1)

        def split_base(eng, ops, runs):
            for r in runs:
                eng.wait_ge(base_hi_ready, r + 1)
                ops.tensor_tensor(base_lo[:, r, :], base_sb[:, r, :],
                                  base_hi[:, r, :].bitcast(F32), ALU.subtract)\
                    .then_inc(base_lo_ready, 1)

        block = ctx.enter_context(nc.Block())

        @block.sync
        def _(sync):
            for h in range(HALVES):
                sync.dma_start(x_in[0][:, h, :, :], x_blocks[0, :, h, :, :]).then_inc(x_loaded[0], 16)
            for r in range(0, RUNS, 2):
                sync.dma_start(base_sb[:, r:r + 2, :], base_w[:, r:r + 2, :])\
                    .then_inc(base_in[r // 2], 16)
            sync.dma_start(x_in[1][:, :, :, :], x_blocks[1]).then_inc(x_loaded[1], 16)
            sync.dma_start(up_sb[:, :], up_w).then_inc(up_in, 16)
            sync.dma_start(xr[0][:, :], x_rows[0]).then_inc(xr_loaded[0], 16)
            sync.dma_start(xr[1][:, :], x_rows[1]).then_inc(xr_loaded[1], 16)
            sync.wait_ge(x_lo_first, HALVES)
            sync.dma_start(x_in[0][:, :, :, :], x_blocks[2]).then_inc(x_loaded[0], 16)

            def step(t, k, p):
                if k % 2 == 0 and up_to_tile(t, TILES - 10):
                    if from_tile(t, 0):
                        sync.wait_ge(x_lo_ready, p + 1)
                    else:
                        sync.wait_ge(x_lo_first, 2 * HALVES)
                    sync.dma_start(x_in[k // 2][:, :, :, :], x_blocks[p + 4])\
                        .then_inc(x_loaded[k // 2], 16)
                if not from_tile(t, 0):
                    return
                if from_tile(t, 1):
                    sync.wait_ge(out_added, t)
                    sync.dma_start(out[t - 1], xr[(k - 1) % XRING][:, :])\
                        .then_inc(stored[(k - 1) % XRING], 16)
                if up_to_tile(t, TILES - 3):
                    if from_tile(t, 2):
                        sync.wait_ge(stored[(k - 2) % XRING], (t - 2 - (k - 2) % XRING) * 4 + 16)
                    sync.dma_start(xr[(k + 2) % XRING][:, :], x_rows[t + 2])\
                        .then_inc(xr_loaded[(k + 2) % XRING], 16)

            each_step(sync, step)
            sync.wait_ge(out_added, TILES)
            sync.dma_start(out[TILES - 1], xr[(TILES - 1) % XRING][:, :])\
                .then_inc(stored[(TILES - 1) % XRING], 16)
            for i in range(XRING):
                sync.wait_ge(stored[i], 16 * (TILES // XRING))

        @block.scalar
        def _(act):
            act.dma_start(conv_sb[:, :, :, :], conv_w).then_inc(conv_w_in, 16)
            act.dma_start(cond_in_sb[:, :], cond).then_inc(cond_in, 16)
            act.wait_ge(zeros_ready, 1)
            nc.scalar.activation(zero_exp[:, :], zeros[:, 0:1], ACT.Exp)
            act.wait_ge(x_loaded[0], 16 * HALVES)
            for h in range(HALVES):
                nc.scalar.activation(x_hi[0][:, h, :, :], x_in[0][:, h, :, :], ACT.Copy)\
                    .then_inc(x_hi_ready, 1)
            for r in range(RUNS):
                act.wait_ge(base_in[r // 2], 16)
                nc.scalar.activation(base_hi[:, r, :], base_sb[:, r, :], ACT.Copy)\
                    .then_inc(base_hi_ready, 1)
            def step(t, k, p):
                if from_tile(t, 0):
                    act.wait_ge(shifted_ready, t + 1)
                    nc.scalar.activation(exps[k % 2][:, :], shifted[k % 2][:, :], ACT.Exp,
                                         accum_out=total[k % 2][:, :]).then_inc(exps_ready, 1)
                if k % 2 == 0 and from_tile(t, 0) and up_to_tile(t, TILES - 6):
                    i = k // 2
                    act.wait_ge(x_loaded[i], (p + 2 - i) * 8 + 16 + (16 if i == 0 else 0))
                    act.wait_ge(conv_done, t + 2)
                    nc.scalar.activation(x_hi[i][:, :, :, :], x_in[i][:, :, :, :], ACT.Copy)\
                        .then_inc(x_hi_ready, 1)
                if from_tile(t, -1) and up_to_tile(t, TILES - 2):
                    if from_tile(t, 1):
                        act.wait_ge(down_done, t)
                        act.wait_ge(y_lo_ready, t)
                    act.wait_ge(turned, t + 2)
                    copy_turned(nc.scalar.copy, t + 1, k + 1, 1, y_odd_ready)
                if from_tile(t, 0):
                    if from_tile(t, 2):
                        act.wait_ge(out_done, t - 1)
                    act.wait_ge(hwt_done, t + 1)
                    nc.scalar.activation(hw_hi[k % 2][:, :], hwt_ps[:, 0:P], ACT.Copy)\
                        .then_inc(hw_hi_ready, 1)
                if from_tile(t, -1) and up_to_tile(t, TILES - 2):
                    act.wait_ge(y_even_ready, 2 * t + 4)
                    act.wait_ge(y_odd_ready, 2 * t + 4)
                    if from_tile(t, 1):
                        act.wait_ge(out_done, t)
                    nc.scalar.activation(y_hi[(k + 1) % 2][:, :, :], y[(k + 1) % 2][:, :, :],
                                         ACT.Copy).then_inc(y_hi_ready, 1)
                if not from_tile(t, 0) and t == -1:
                    act.wait_ge(x_loaded[1], 16)
                    nc.scalar.activation(x_hi[1][:, :, :, :], x_in[1][:, :, :, :], ACT.Copy)\
                        .then_inc(x_hi_ready, 1)
                    act.wait_ge(up_in, 16)
                    nc.scalar.activation(up_hi[:, :], up_sb[:, :], ACT.Copy,
                                         scale=LORA_SCALE).then_inc(up_hi_ready, 1)

            each_step(act, step)

        @block.gpsimd
        def _(pool):
            nc.gpsimd.memset(zeros[:, :], 0.0).then_inc(zeros_ready, 1)
            nc.gpsimd.memset(ident[:, :], 0.0).then_inc(ident_zeroed, 1)
            pool.wait_ge(ident_zeroed, 1)
            nc.gpsimd.affine_select(out=ident[:, :], in_=ident[:, :], compare_op=ALU.not_equal,
                                    fill=1.0, base=0, pattern=[[-1, P]], channel_multiplier=1)\
                .then_inc(ident_ready, 1)
            pool.dma_start(map_i[:, :], expert_map.partition_broadcast(P)).then_inc(map_in, 16)
            pool.dma_start(down_sb[:, :, :], down_w).then_inc(down_in, 16)
            pool.dma_start(biases_sb[:, :], biases.partition_broadcast(P)).then_inc(biases_in, 16)
            split_base(pool, nc.gpsimd, range(RUNS // 2))
            pool.wait_ge(biases_in, 16)

            def bias_rows(t, k):
                pool.wait_ge(xr_loaded[k], (t - k) * 4 + 16)
                nc.gpsimd.tensor_tensor(xr[k][:, :], xr[k][:, :], base_b_sb[:, :], ALU.add)\
                    .then_inc(xr_biased, 1)

            def step(t, k, p):
                if k % 2 == 0 and from_tile(t, 0) and up_to_tile(t, TILES - 6):
                    i = k // 2
                    pool.wait_ge(x_hi_ready, p + 3 + 1)
                    nc.gpsimd.tensor_tensor(x_lo[i][:, :, :, :], x_in[i][:, :, :, :],
                                            x_hi[i][:, :, :, :].bitcast(F32), ALU.subtract)\
                        .then_inc(x_lo_ready, 1)
                if from_tile(t, -1) and up_to_tile(t, TILES - 2):
                    if from_tile(t, 0):
                        bias_rows(t + 1, (k + 1) % XRING)
                    pool.wait_ge(y_hi_ready, t + 2)
                    nc.gpsimd.tensor_tensor(y_lo[(k + 1) % 2][:, :, :], y[(k + 1) % 2][:, :, :],
                                            y_hi[(k + 1) % 2][:, :, :].bitcast(F32), ALU.subtract)\
                        .then_inc(y_lo_ready, 1)
                    if not from_tile(t, 0):
                        bias_rows(t + 1, (k + 1) % XRING)

            each_step(pool, step)

        @block.tensor
        def _(pe):
            pe.wait_ge(zeros_ready, 1)
            for n in range(WARM_UP):
                nc.tensor.matmul(turn_ps[:, :, :, :, :].rearrange("p a h r o -> p (a h r o)"),
                                 zeros[:, 0:P], zeros[:, :], start=True, stop=True)
            pe.wait_ge(cond_in, 16)
            for h in range(HALVES):
                mm = nc.tensor.matmul(cond_ps[:, h, :], cond_w_sb[:, h, :], cond_t_sb[:, :],
                                      start=True, stop=True)
            mm.then_inc(cond_summed, 1)

            def conv(t, k, p):
                i, h = (k // 2 + 1) % 2, k % 2
                if from_tile(t, 0):
                    pe.wait_ge(y_rows_ready, t + 1)
                if from_tile(t, 2):
                    pe.wait_ge(x_lo_ready, p)
                else:
                    pe.wait_ge(conv_lo_ready, k % 2 + 1)
                    pe.wait_ge(x_lo_first, t + 3)
                n = 0
                for b in range(BLOCKS):
                    for w, a in ((conv_hi, x_hi), (conv_lo, x_hi), (conv_hi, x_lo)):
                        mm = nc.tensor.matmul(conv_ps[h][:, :, :], w[:, h, b, :],
                                              a[i][:, h, :, b:b + M], start=n == 0,
                                              stop=n == 3 * BLOCKS - 1)
                        n += 1
                mm.then_inc(conv_done, 1)

            def turn(t, k, p):
                i = (k // 2) % 2
                pe.wait_ge(y_rows_ready, t + 2 - k % 2)
                if from_tile(t, 1):
                    pe.wait_ge(y_even_ready, 2 * t)
                    pe.wait_ge(y_odd_ready, 2 * t)
                for a in range(Q // 2):
                    for h in range(HALVES):
                        first = Q * (k % 2) + 2 * a
                        mm = nc.tensor.transpose(
                            turn_ps[:, a, h, :, :].rearrange("p r o -> p (r o)"),
                            y_rows[i][:, h, first:first + 2, :].rearrange("p n m -> p (n m)"),
                            ident[:, :])
                mm.then_inc(turned, 1)

            def down(t, k):
                pe.wait_ge(y_even_ready, 2 * t + 2)
                pe.wait_ge(y_odd_ready, 2 * t + 2)
                if from_tile(t, 2):
                    pe.wait_ge(hw_ready, t - 1)
                for r in range(RUNS):
                    mm = nc.tensor.matmul(down_ps[k % 2][:, 0:HL], y[k % 2][:, r, :],
                                          down_sb[:, r, :], start=r == 0, stop=r == RUNS - 1)
                mm.then_inc(down_done, 1)

            def linear(t, k, runs):
                for r in runs:
                    for n, (a, w) in enumerate(((y_hi, base_hi), (y_hi, base_lo), (y_lo, base_hi))):
                        nc.tensor.matmul(out_ps[k % 2][:, :], a[k % 2][:, r, :], w[:, r, :],
                                         start=r == 0 and n == 0, stop=False)

            def step(t, k, p):
                if up_to_tile(t, TILES - 3):
                    conv(t, k, p)
                if not from_tile(t, -1):
                    return
                if not from_tile(t, 0):
                    pe.wait_ge(ident_ready, 1)
                    turn(t + 1, k + 1, p + 1)
                    pe.wait_ge(down_in, 16)
                    down(t + 1, k + 1)
                    pe.wait_ge(base_lo_ready, RUNS)
                    return
                if from_tile(t, 2):
                    pe.wait_ge(out_added, t - 1)
                pe.wait_ge(y_lo_ready, t + 1)
                linear(t, k, range(RUNS // 2))
                if up_to_tile(t, TILES - 2):
                    turn(t + 1, k + 1, p)
                linear(t, k, range(RUNS // 2, RUNS - 1))
                if from_tile(t, 1):
                    pe.wait_ge(hw_lo_ready, t)
                pe.wait_ge(hw_ready, t + 1)
                nc.tensor.transpose(hwt_ps[:, 0:P], hw[k % 2][:, :], ident[:, :])\
                    .then_inc(hwt_done, 1)
                linear(t, k, range(RUNS - 1, RUNS))
                if up_to_tile(t, TILES - 2):
                    if not from_tile(t, 1):
                        pe.wait_ge(cond_biased, HALVES)
                        pe.wait_ge(up_lo_ready, 1)
                    down(t + 1, k + 1)
                pe.wait_ge(hw_hi_ready, t + 1)
                nc.tensor.matmul(out_ps[k % 2][:, :], hw_hi[k % 2][:, :], up_hi[:, :],
                                 start=False, stop=False)
                nc.tensor.matmul(out_ps[k % 2][:, :], hw_hi[k % 2][:, :], up_lo[:, :],
                                 start=False, stop=False)
                pe.wait_ge(hw_lo_ready, t + 1)
                nc.tensor.matmul(out_ps[k % 2][:, :], hw_lo[k % 2][:, :], up_hi[:, :],
                                 start=False, stop=True).then_inc(out_done, 1)

            each_step(pe, step)

        @block.vector
        def _(dve):
            dve.wait_ge(conv_w_in, 16)
            for h in range(HALVES):
                nc.vector.tensor_copy(conv_hi[:, h, :, :], conv_sb[:, h, :, :])\
                    .then_inc(conv_hi_ready, 1)
                dve.wait_ge(conv_hi_ready, h + 1)
                nc.vector.tensor_tensor(conv_lo[:, h, :, :], conv_sb[:, h, :, :],
                                        conv_hi[:, h, :, :].bitcast(F32), ALU.subtract)\
                    .then_inc(conv_lo_ready, 1)
            for h in range(HALVES):
                dve.wait_ge(x_hi_ready, h + 1)
                nc.vector.tensor_tensor(x_lo[0][:, h, :, :], x_in[0][:, h, :, :],
                                        x_hi[0][:, h, :, :].bitcast(F32), ALU.subtract)\
                    .then_inc(x_lo_first, 1)
            dve.wait_ge(cond_summed, 1)
            for h in range(HALVES):
                nc.vector.tensor_scalar(cond_sb[:, h, :], cond_ps[:, h, :], conv_b_sb[:, h:h + 1],
                                        None, ALU.add).then_inc(cond_biased, 1)
            dve.wait_ge(cond_biased, HALVES)

            def split_up():
                dve.wait_ge(up_hi_ready, 1)
                nc.vector.scalar_tensor_tensor(out=up_lo[:, :], in0=up_sb[:, :], scalar=LORA_SCALE,
                                               in1=up_hi[:, :].bitcast(F32), op0=ALU.mult,
                                               op1=ALU.subtract).then_inc(up_lo_ready, 1)

            def read_map():
                dve.wait_ge(map_in, 16)
                nc.vector.tensor_copy(map_f[:, :], map_i[:, :]).then_inc(map_ready, 1)
                dve.wait_ge(map_ready, 1)
                for e in range(E):
                    nc.vector.tensor_scalar(is_expert[:, e, :], map_f[:, :], float(e), None,
                                            ALU.is_equal).then_inc(map_ready, 1)
                dve.wait_ge(map_ready, 1 + E)

            def add_out(t, k):
                dve.wait_ge(xr_biased, t + 1)
                dve.wait_ge(out_done, t + 1)
                nc.vector.tensor_tensor(xr[k][:, :], out_ps[k % 2][:, :], xr[k][:, :], ALU.add)\
                    .then_inc(out_added, 1)

            def condition(t, k, p):
                i, h = (k // 2 + 1) % 2, k % 2
                if from_tile(t, 2):
                    dve.wait_ge(turned, t - k % 2)
                dve.wait_ge(conv_done, t + 3)
                c = cond_sb[:, h, bass.ds((p + 1) * PAIR, PAIR)]
                nc.vector.tensor_tensor(y_rows[i][:, h, :, :], conv_ps[h][:, :, :],
                                        c.unsqueeze(2).to_broadcast([P, PAIR, M]), ALU.add)\
                    .then_inc(y_rows_ready, 1)

            def choose(t, k):
                i = k % 2
                dve.wait_ge(down_done, t + 1)
                nc.vector.tensor_tensor(logits[i][:, :], down_ps[i][:, E * R:HL],
                                        router_b_sb[:, :], ALU.add).then_inc(logits_ready, 1)
                dve.wait_ge(logits_ready, t + 1)
                nc.vector.tensor_reduce(best[i][:, :], logits[i][:, :], AX_X, ALU.max)\
                    .then_inc(best_ready, 1)
                nc.vector.max(top[i][:, :], logits[i][:, :]).then_inc(top_ready, 1)
                dve.wait_ge(top_ready, t + 1)
                dve.wait_ge(best_ready, t + 1)
                nc.vector.tensor_scalar(shifted[i][:, :], logits[i][:, :], best[i][:, 0:1], None,
                                        ALU.subtract).then_inc(shifted_ready, 1)
                nc.vector.match_replace(rest[i][:, :], top[i][:, :], logits[i][:, :], LOWEST)\
                    .then_inc(rest_ready, 1)
                dve.wait_ge(rest_ready, t + 1)
                nc.vector.tensor_tensor(chosen[i][:, :], rest[i][:, :], logits[i][:, :],
                                        ALU.not_equal).then_inc(chosen_ready, 1)

            def weigh_routes(t, k):
                i = k % 2
                dve.wait_ge(exps_ready, t + 1)
                nc.vector.reciprocal(inv[i][:, :], total[i][:, :]).then_inc(inv_ready, 1)
                dve.wait_ge(chosen_ready, t + 1)
                dve.wait_ge(inv_ready, t + 1)
                nc.vector.scalar_tensor_tensor(out=weight[i][:, :], in0=exps[i][:, :],
                                               scalar=inv[i][:, 0:1], in1=chosen[i][:, :],
                                               op0=ALU.mult, op1=ALU.mult).then_inc(weight_ready, 1)

            def weigh_experts(t, k):
                i = k % 2
                dve.wait_ge(weight_ready, t + 1)
                nc.vector.tensor_tensor(spread[i][:, :, :], is_expert[:, :, :],
                                        weight[i][:, :].unsqueeze(1).to_broadcast([P, E, ROUTES]),
                                        ALU.mult).then_inc(spread_ready, 1)
                dve.wait_ge(spread_ready, t + 1)
                nc.vector.tensor_reduce(expert_w[i][:, :], spread[i][:, :, :], AX_X, ALU.add)\
                    .then_inc(expert_w_ready, 1)
                if from_tile(t, 2):
                    dve.wait_ge(hwt_done, t - 1)
                dve.wait_ge(expert_w_ready, t + 1)
                nc.vector.tensor_tensor(
                    hw[i][:, :].rearrange("p (e r) -> p e r", e=E),
                    down_ps[i][:, 0:E * R].rearrange("p (e r) -> p e r", e=E),
                    expert_w[i][:, :].unsqueeze(2).to_broadcast([P, E, R]),
                    ALU.mult).then_inc(hw_ready, 1)

            def step(t, k, p):
                if from_tile(t, 0):
                    choose(t, k)
                if from_tile(t, 1):
                    add_out(t - 1, (k - 1) % UNROLL)
                if from_tile(t, 0):
                    weigh_routes(t, k)
                if up_to_tile(t, TILES - 3):
                    condition(t, k, p)
                if from_tile(t, 0):
                    weigh_experts(t, k)
                elif t == -1:
                    split_base(dve, nc.vector, range(RUNS // 2, RUNS))
                if from_tile(t, -1) and up_to_tile(t, TILES - 2):
                    if from_tile(t, 1):
                        dve.wait_ge(down_done, t)
                        dve.wait_ge(y_lo_ready, t)
                    dve.wait_ge(turned, t + 2)
                    copy_turned(nc.vector.tensor_copy, t + 1, k + 1, 0, y_even_ready)
                if from_tile(t, 0):
                    dve.wait_ge(hw_hi_ready, t + 1)
                    if from_tile(t, 2):
                        dve.wait_ge(out_done, t - 1)
                    nc.vector.tensor_tensor(hw_lo[k % 2][:, :], hwt_ps[:, 0:P],
                                            hw_hi[k % 2][:, :].bitcast(F32), ALU.subtract)\
                        .then_inc(hw_lo_ready, 1)
                elif t == -1:
                    dve.wait_ge(x_hi_ready, HALVES + 1)
                    for h in range(HALVES):
                        nc.vector.tensor_tensor(x_lo[1][:, h, :, :], x_in[1][:, h, :, :],
                                                x_hi[1][:, h, :, :].bitcast(F32), ALU.subtract)\
                            .then_inc(x_lo_first, 1)
                    split_up()
                    dve.wait_ge(biases_in, 16)

            read_map()
            each_step(dve, step)
            add_out(TILES - 1, (TILES - 1) % UNROLL)


def kernel(x, cond_128, fside_S_0, L0_cond_weight, L0_cond_c_weight, L0_ffn_base_W, L0_ffn_base_b,
           L0_ffn_router_W, L0_ffn_router_b, L0_ffn_A, L0_ffn_B, L0_ffn_expert_map):
    import numpy as np
    from concourse import bacc
    from concourse.bass_utils import run_bass_kernel_spmd

    def in_turn_order(a):
        return np.asarray(a).reshape(TILES, 2, Q // 2, -1).transpose(0, 2, 1, 3).reshape(a.shape)

    x = np.asarray(x)
    per = C // GROUPS
    blocks = np.pad(in_turn_order(x), ((0, 0), (0, 0), (PAD, BP - PAD)))
    blocks = blocks.reshape(N // PAIR, PAIR, HALVES, CH, MI, BP).transpose(0, 5, 3, 2, 1, 4)

    w = np.asarray(L0_cond_weight)
    conv = np.zeros((BP, CH, HALVES, BLOCKS, BP, CH), w.dtype)
    for b in range(BLOCKS):
        for s in range(BP):
            for r in range(BP):
                tap = BP * b + s - r
                if 0 <= tap < TAPS:
                    for g in range(GROUPS):
                        h, own = g * per // CH, slice(g * per % CH, g * per % CH + per)
                        conv[s, own, h, b, r, own] = w[g * per:(g + 1) * per, :, tap].T

    def by_output_row(a):
        a = np.asarray(a).reshape(HALVES, CH, -1)
        return np.stack([a] * BP).transpose(0, 2, 1, 3).reshape(P, HALVES, -1)

    def by_position(a):
        a = np.asarray(a).reshape(-1, M, 2, RUNS)
        return a.transpose(2, 1, 3, 0).reshape(P, RUNS, -1)

    down = np.concatenate([by_position(L0_ffn_A), by_position(L0_ffn_router_W)], axis=2)
    given = {
        "x_blocks": blocks.reshape(N // PAIR, P, HALVES, PAIR, MI),
        "x_rows": x.reshape(TILES, P, L),
        "conv_w": conv.reshape(P, HALVES, BLOCKS, P),
        "cond": np.concatenate([in_turn_order(cond_128).T,
                                by_output_row(L0_cond_c_weight).transpose(2, 1, 0).reshape(P, -1),
                                by_output_row(fside_S_0).reshape(P, HALVES)], axis=1),
        "base_w": by_position(L0_ffn_base_W),
        "down_w": down,
        "up_w": np.asarray(L0_ffn_B).transpose(0, 2, 1).reshape(E * R, L),
        "biases": np.concatenate([L0_ffn_base_b, L0_ffn_router_b]),
        "expert_map": L0_ffn_expert_map,
    }
    nc = bacc.Bacc("TRN2", target_bir_lowering=False, num_devices=1)
    arrays, args = {}, []
    for name, a in given.items():
        a = np.ascontiguousarray(a)
        arrays[name] = a
        args.append(nc.dram_tensor(name, a.shape, mybir.dt.from_np(a.dtype), kind="ExternalInput").ap())
    out = nc.dram_tensor("out", (TILES, P, L), F32, kind="ExternalOutput").ap()
    build(nc, *args, out)
    r = run_bass_kernel_spmd(nc, [arrays], core_ids=[0])
    return r.results[0]["out"].reshape(N, C, L)
```

```python
from contextlib import ExitStack

import concourse.bass as bass
from concourse import mybir

F32 = mybir.dt.float32
BF16 = mybir.dt.bfloat16
F32R = mybir.dt.float32r
I32 = mybir.dt.int32
ALU = mybir.AluOpType
ACT = mybir.ActivationFunctionType
AX_X = mybir.AxisListType.X

P = 128
N, C, L = 128, 32, 512
TAPS, GROUPS, PAD = 9, 4, 4
E, R = 8, 16
ROUTES = 2 * E - 1
TOP = E
LORA_SCALE = 32.0 / 16.0
LOWEST = -3.0e38

Q = P // C
TILES = N // Q
HALVES = 2
CH = C // HALVES
PAIR = 2 * Q
BP = P // CH
M = L // BP
MI = M + 1
BLOCKS = 2
MK = M // 2
TERMS = 3
START = 2
RUNS = BP // 2
HR = E * R
FRONT = HR + ROUTES + 1
WIDE = FRONT + L
BANK = 512
HALF = L // 2

XRING = 4
UNROLL = 4
WARM_UP, WARM_BETWEEN, WARM_END = 9, 7, 4


def build(nc, x_start, x_even, x_odd, x_rows, conv_w, cond, wide_w, up_w, biases, expert_map, out):
    ctx = ExitStack()
    with ctx:
        def sb(name, shape, dt=F32):
            return ctx.enter_context(nc.sbuf_tensor(name, shape, dt))

        def pb(name, shape):
            return ctx.enter_context(nc.psum_tensor(name, shape, F32))

        def sem(name):
            return ctx.enter_context(nc.semaphore(name))

        conv_sb = sb("conv_sb", [P, HALVES, BLOCKS, P])
        conv_sum = sb("conv_sum", [P, HALVES, P])
        conv_hi = sb("conv_hi", [P, HALVES, BLOCKS + 1, P], F32R)
        conv_lo = sb("conv_lo", [P, HALVES, BLOCKS + 1, P], F32R)
        cond_in_sb = sb("cond_in_sb", [P, N + HALVES * P + HALVES])
        cond_t_sb = cond_in_sb[:, 0:N]
        cond_w_sb = cond_in_sb[:, N:N + HALVES * P].rearrange("p (h q) -> p h q", h=HALVES)
        conv_b_sb = cond_in_sb[:, N + HALVES * P:]
        cond_sb = sb("cond_sb", [P, HALVES, N])
        wide_sb = sb("wide_sb", [P, RUNS, WIDE])
        wide_hi = sb("wide_hi", [P, RUNS, WIDE], F32R)
        wide_lo = sb("wide_lo", [P, RUNS, WIDE], F32R)
        biases_sb = sb("biases_sb", [P, L + ROUTES])
        base_b_sb = biases_sb[:, 0:L]
        router_b_sb = biases_sb[:, L:]
        up_sb = sb("up_sb", [P, L])
        up_scaled = sb("up_scaled", [P, L])
        up_hi = sb("up_hi", [P, L], F32R)
        up_lo = sb("up_lo", [P, L], F32R)
        map_i = sb("map_i", [P, ROUTES], I32)
        map_f = sb("map_f", [P, ROUTES])
        is_expert = sb("is_expert", [P, E, ROUTES])
        ident = sb("ident", [P, P])
        zeros = sb("zeros", [P, L], BF16)
        zero_exp = sb("zero_exp", [P, 1])

        x_in = [sb(f"x_in{i}", [P, HALVES, PAIR, MI]) for i in range(START)]
        x_hi = [sb(f"x_hi{i}", [P, HALVES, PAIR, MI], F32R) for i in range(START)]
        x_lo = [sb(f"x_lo{i}", [P, HALVES, PAIR, MI], F32R) for i in range(START)]
        even = [sb(f"even{i}", [P, HALVES, PAIR, MK + 1]) for i in range(2)]
        terms = [sb(f"terms{i}", [P, HALVES, TERMS, PAIR, MK]) for i in range(2)]
        terms_hi = [sb(f"terms_hi{i}", [P, HALVES, TERMS, PAIR, MK], F32R) for i in range(2)]
        terms_lo = [sb(f"terms_lo{i}", [P, HALVES, TERMS, PAIR, MK], F32R) for i in range(2)]
        common = sb("common", [P, PAIR, MK])
        y_rows = [sb(f"y_rows{i}", [P, HALVES, PAIR, M]) for i in range(2)]
        xr = [sb(f"xr{i}", [P, L]) for i in range(XRING)]
        y = [sb(f"y{i}", [P, RUNS, P]) for i in range(2)]
        y_hi = [sb(f"y_hi{i}", [P, RUNS, P], F32R) for i in range(2)]
        y_lo = [sb(f"y_lo{i}", [P, RUNS, P], F32R) for i in range(2)]
        logits = [sb(f"logits{i}", [P, ROUTES]) for i in range(2)]
        best = [sb(f"best{i}", [P, 1]) for i in range(2)]
        top = [sb(f"top{i}", [P, TOP]) for i in range(2)]
        shifted = [sb(f"shifted{i}", [P, ROUTES]) for i in range(2)]
        exps = [sb(f"exps{i}", [P, ROUTES]) for i in range(2)]
        total = [sb(f"total{i}", [P, 1]) for i in range(2)]
        inv = [sb(f"inv{i}", [P, 1]) for i in range(2)]
        rest = [sb(f"rest{i}", [P, ROUTES]) for i in range(2)]
        chosen = [sb(f"chosen{i}", [P, ROUTES]) for i in range(2)]
        weight = [sb(f"weight{i}", [P, ROUTES]) for i in range(2)]
        spread = [sb(f"spread{i}", [P, E, ROUTES]) for i in range(2)]
        expert_w = [sb(f"expert_w{i}", [P, E]) for i in range(2)]
        hw = [sb(f"hw{i}", [P, E * R]) for i in range(2)]
        hw_hi = [sb(f"hw_hi{i}", [P, P], F32R) for i in range(2)]
        hw_lo = [sb(f"hw_lo{i}", [P, P], F32R) for i in range(2)]

        conv_banks = pb("conv_banks", [P, 2, BANK])
        conv_ps = conv_banks[:, :, :].rearrange("p h (n m) -> p h n m", m=M)
        own_ps = conv_banks[:, 0, :].rearrange("p (a n k) -> p a n k", a=2, k=MK)
        common_ps = conv_banks[:, 1, 0:PAIR * MK].rearrange("p (n k) -> p n k", k=MK)
        turn_ps = pb("turn_ps", [P, Q // 2, HALVES, BP, CH])
        hwt_ps = pb("hwt_ps", [P, BANK])
        wide_ps = [pb(f"wide_ps{i}", [P, 2, BANK]) for i in range(2)]
        first_ps = wide_ps[0][:, :, 0:Q * M].rearrange("p h (n m) -> p h n m", m=M)
        cond_ps = hwt_ps[:, 0:HALVES * N].rearrange("p (h n) -> p h n", h=HALVES)

        conv_w_in = sem("conv_w_in")
        cond_in = sem("cond_in")
        wide_in = [sem(f"wide_in{i}") for i in range(RUNS // 2)]
        up_in = sem("up_in")
        biases_in = sem("biases_in")
        map_in = sem("map_in")
        zeros_ready = sem("zeros_ready")
        conv_hi_ready = sem("conv_hi_ready")
        conv_lo_ready = sem("conv_lo_ready")
        conv_summed = sem("conv_summed")
        conv_sum_hi_ready = sem("conv_sum_hi_ready")
        conv_sum_lo_ready = sem("conv_sum_lo_ready")
        x_first_in = sem("x_first_in")
        x_second_in = sem("x_second_in")
        x_third_in = sem("x_third_in")
        x_hi_first = sem("x_hi_first")
        x_hi_ready = sem("x_hi_ready")
        x_lo_first = sem("x_lo_first")
        y_rows_first = sem("y_rows_first")
        cond_summed = sem("cond_summed")
        cond_biased = sem("cond_biased")
        wide_hi_ready = sem("wide_hi_ready")
        wide_lo_ready = sem("wide_lo_ready")
        up_scaled_ready = sem("up_scaled_ready")
        up_hi_ready = sem("up_hi_ready")
        up_lo_ready = sem("up_lo_ready")
        map_ready = sem("map_ready")
        ident_zeroed = sem("ident_zeroed")
        ident_ready = sem("ident_ready")
        terms_loaded = [sem(f"terms_loaded{i}") for i in range(2)]
        xr_loaded = [sem(f"xr_loaded{i}") for i in range(XRING)]
        stored = [sem(f"stored{i}") for i in range(XRING)]
        differences_ready = sem("differences_ready")
        terms_hi_ready = sem("terms_hi_ready")
        terms_lo_ready = sem("terms_lo_ready")
        common_done = sem("common_done")
        common_ready = sem("common_ready")
        conv_done = sem("conv_done")
        y_rows_ready = sem("y_rows_ready")
        turned = sem("turned")
        y_even_ready = sem("y_even_ready")
        y_odd_ready = sem("y_odd_ready")
        y_hi_ready = sem("y_hi_ready")
        y_lo_ready = sem("y_lo_ready")
        front_done = sem("front_done")
        linear_done = sem("linear_done")
        logits_ready = sem("logits_ready")
        top_ready = sem("top_ready")
        best_ready = sem("best_ready")
        shifted_ready = sem("shifted_ready")
        exps_ready = sem("exps_ready")
        inv_ready = sem("inv_ready")
        rest_ready = sem("rest_ready")
        chosen_ready = sem("chosen_ready")
        weight_ready = sem("weight_ready")
        spread_ready = sem("spread_ready")
        expert_w_ready = sem("expert_w_ready")
        hw_ready = sem("hw_ready")
        hwt_done = sem("hwt_done")
        hw_hi_ready = sem("hw_hi_ready")
        hw_lo_ready = sem("hw_lo_ready")
        out_done = sem("out_done")
        xr_biased = sem("xr_biased")
        out_added = sem("out_added")

        def each_step(eng, step):
            for t in range(UNROLL):
                step(t, t % UNROLL, t // 2)
            with eng.Fori(1, TILES // UNROLL - 2) as group:
                for k in range(UNROLL):
                    step(group * UNROLL + k, k, group * (UNROLL // 2) + k // 2)
            for t in range(TILES - 2 * UNROLL, TILES + 1):
                step(t, t % UNROLL, t // 2)

        def from_tile(t, least):
            return not isinstance(t, int) or t >= least

        def up_to_tile(t, most):
            return not isinstance(t, int) or t <= most

        def copy_turned(copy, t, k, j, ready):
            for low in range(2):
                src = turn_ps[j * M:(j + 1) * M, :, :, low * RUNS:(low + 1) * RUNS, :]
                dst = y[k % 2][low * M:(low + 1) * M, :, j * (P // 2):(j + 1) * (P // 2)]
                copy(dst.rearrange("m r (a o) -> m a r o", o=CH),
                     src.rearrange("m a h r o -> m (a h) r o")).then_inc(ready, 1)

        def split_wide(eng, ops, runs):
            for r in runs:
                eng.wait_ge(wide_hi_ready, r + 1)
                ops.tensor_tensor(wide_lo[:, r, :], wide_sb[:, r, :],
                                  wide_hi[:, r, :].bitcast(F32), ALU.subtract)\
                    .then_inc(wide_lo_ready, 1)

        def sums_of(t, k):
            if isinstance(t, int) and t >= TILES - 2:
                return conv_banks[:, :, :] if t == TILES - 2 else wide_ps[0][:, :, :]
            return wide_ps[k % 2][:, :, :]

        def linear_sums(t, k):
            flat = sums_of(t, k).rearrange("p b n -> p (b n)")
            return flat[:, FRONT:FRONT + 2 * (BANK - FRONT)]\
                .rearrange("p (b n) -> p b n", b=2)[:, :, 0:HALF]

        block = ctx.enter_context(nc.Block())

        @block.sync
        def _(sync):
            sync.dma_start(x_in[0][:, :, 0:Q, :], x_start[0, :, :, 0:Q, :])\
                .then_inc(x_first_in, 16)
            sync.dma_start(conv_sb[:, :, :, :], conv_w).then_inc(conv_w_in, 16)
            sync.dma_start(cond_in_sb[:, :], cond).then_inc(cond_in, 16)
            sync.dma_start(x_in[0][:, :, Q:, :], x_start[0, :, :, Q:, :]).then_inc(x_second_in, 16)
            for r in range(0, RUNS, 2):
                sync.dma_start(wide_sb[:, r:r + 2, :], wide_w[:, r:r + 2, :])\
                    .then_inc(wide_in[r // 2], 16)
            sync.dma_start(x_in[1][:, :, :, :], x_start[1]).then_inc(x_third_in, 16)
            sync.dma_start(up_sb[:, :], up_w).then_inc(up_in, 16)
            sync.dma_start(xr[0][:, :], x_rows[0]).then_inc(xr_loaded[0], 16)
            sync.dma_start(xr[1][:, :], x_rows[1]).then_inc(xr_loaded[1], 16)

            def load_terms(q, i):
                sync.dma_start(even[i][:, :, :, :], x_even[q - START])\
                    .then_inc(terms_loaded[i], 16)
                sync.dma_start(terms[i][:, :, TERMS - 1, :, :], x_odd[q - START])\
                    .then_inc(terms_loaded[i], 16)

            load_terms(2, 0)
            load_terms(3, 1)

            def step(t, k, p):
                if from_tile(t, 2):
                    sync.wait_ge(out_added, t - 1)
                    sync.dma_start(out[t - 2], xr[(k - 2) % XRING][:, :])\
                        .then_inc(stored[(k - 2) % XRING], 16)
                if from_tile(t, 1) and up_to_tile(t, TILES - 2):
                    i = (k + 1) % XRING
                    if from_tile(t, 3):
                        sync.wait_ge(stored[i], (t - 3 - i) * 4 + 16)
                    sync.dma_start(xr[i][:, :], x_rows[t + 1]).then_inc(xr_loaded[i], 16)
                if k % 2 == 0 and up_to_tile(t, TILES - 10):
                    sync.wait_ge(terms_lo_ready, p + 1)
                    load_terms(p + 4, k // 2)

            each_step(sync, step)
            last = (TILES - 1) % XRING
            for b in range(2):
                columns = slice(b * HALF, (b + 1) * HALF)
                sync.wait_ge(out_added, TILES + b)
                sync.dma_start(out[TILES - 1, :, columns], xr[last][:, columns])\
                    .then_inc(stored[last], 16)
            for i in range(XRING):
                sync.wait_ge(stored[i], 16 * (TILES // XRING + (1 if i == last else 0)))

        @block.scalar
        def _(act):
            act.wait_ge(zeros_ready, 1)
            nc.scalar.activation(zero_exp[:, :], zeros[:, 0:1], ACT.Exp)
            act.wait_ge(conv_w_in, 16)
            for h in range(HALVES):
                nc.scalar.activation(conv_hi[:, h, 0:BLOCKS, :], conv_sb[:, h, :, :], ACT.Copy)\
                    .then_inc(conv_hi_ready, 1)
            act.wait_ge(conv_summed, 1)
            nc.scalar.activation(conv_hi[:, :, BLOCKS, :], conv_sum[:, :, :], ACT.Copy)\
                .then_inc(conv_sum_hi_ready, 1)
            act.wait_ge(x_second_in, 16)
            nc.scalar.activation(x_hi[0][:, :, Q:, :], x_in[0][:, :, Q:, :], ACT.Copy)\
                .then_inc(x_hi_ready, 1)

            def wide_high(runs):
                for r in runs:
                    act.wait_ge(wide_in[r // 2], 16)
                    nc.scalar.activation(wide_hi[:, r, :], wide_sb[:, r, :], ACT.Copy)\
                        .then_inc(wide_hi_ready, 1)

            def exponentials(t, k):
                act.wait_ge(shifted_ready, t + 1)
                nc.scalar.activation(exps[k % 2][:, :], shifted[k % 2][:, :], ACT.Exp,
                                     accum_out=total[k % 2][:, :]).then_inc(exps_ready, 1)

            def terms_high(q, i, t):
                act.wait_ge(differences_ready, 2 * q - 2)
                if from_tile(t, 3):
                    act.wait_ge(conv_done, t + 2)
                for h in range(HALVES):
                    nc.scalar.activation(terms_hi[i][:, h, :, :, :], terms[i][:, h, :, :, :],
                                         ACT.Copy).then_inc(terms_hi_ready, 1)

            def y_odd(t, k):
                if from_tile(t, 2):
                    act.wait_ge(y_lo_ready, t - 1)
                act.wait_ge(turned, t + 1)
                copy_turned(nc.scalar.copy, t, k, 1, y_odd_ready)

            def y_high(t, k):
                act.wait_ge(y_even_ready, 2 * t + 2)
                act.wait_ge(y_odd_ready, 2 * t + 2)
                if from_tile(t, 2):
                    act.wait_ge(linear_done, t - 1)
                nc.scalar.activation(y_hi[k % 2][:, :, :], y[k % 2][:, :, :], ACT.Copy)\
                    .then_inc(y_hi_ready, 1)

            def hw_high(t, k):
                if from_tile(t, 2):
                    act.wait_ge(out_done, t - 1)
                act.wait_ge(hwt_done, t + 1)
                nc.scalar.activation(hw_hi[k % 2][:, :], hwt_ps[:, 0:P], ACT.Copy)\
                    .then_inc(hw_hi_ready, 1)

            wide_high(range(RUNS // 2))
            y_odd(0, 0)
            y_high(0, 0)
            wide_high(range(RUNS // 2, RUNS))
            act.wait_ge(x_third_in, 16)
            nc.scalar.activation(x_hi[1][:, :, :, :], x_in[1][:, :, :, :], ACT.Copy)\
                .then_inc(x_hi_ready, 1)

            def step(t, k, p):
                if isinstance(t, int) and t == 0:
                    act.wait_ge(up_in, 16)
                    nc.scalar.activation(up_scaled[:, :], up_sb[:, :], ACT.Copy,
                                         scale=LORA_SCALE).then_inc(up_scaled_ready, 1)
                    act.wait_ge(up_scaled_ready, 1)
                    nc.scalar.activation(up_hi[:, :], up_scaled[:, :], ACT.Copy)\
                        .then_inc(up_hi_ready, 1)
                    y_odd(1, 1)
                    y_high(1, 1)
                    terms_high(2, 0, t)
                    exponentials(0, 0)
                    return
                if k % 2 == 0 and up_to_tile(t, TILES - 6):
                    terms_high(p + 2, k // 2, t)
                if isinstance(t, int) and t == TILES - 2:
                    y_odd(t + 1, k + 1)
                    y_high(t + 1, k + 1)
                    hw_high(t - 1, k - 1)
                else:
                    if up_to_tile(t, TILES - 3):
                        y_odd(t + 1, k + 1)
                    hw_high(t - 1, k - 1)
                    if up_to_tile(t, TILES - 3):
                        y_high(t + 1, k + 1)
                if up_to_tile(t, TILES - 1):
                    exponentials(t, k)

            each_step(act, step)

        @block.gpsimd
        def _(pool):
            nc.gpsimd.memset(zeros[:, :], 0.0).then_inc(zeros_ready, 1)
            nc.gpsimd.memset(ident[:, :], 0.0).then_inc(ident_zeroed, 1)
            pool.wait_ge(ident_zeroed, 1)
            nc.gpsimd.affine_select(out=ident[:, :], in_=ident[:, :], compare_op=ALU.not_equal,
                                    fill=1.0, base=0, pattern=[[-1, P]], channel_multiplier=1)\
                .then_inc(ident_ready, 1)
            pool.dma_start(map_i[:, :], expert_map.partition_broadcast(P)).then_inc(map_in, 16)
            pool.wait_ge(conv_w_in, 16)
            nc.gpsimd.tensor_tensor(conv_sum[:, :, :], conv_sb[:, :, 0, :], conv_sb[:, :, 1, :],
                                    ALU.add).then_inc(conv_summed, 1)
            pool.wait_ge(conv_sum_hi_ready, 1)
            nc.gpsimd.tensor_tensor(conv_lo[:, :, BLOCKS, :], conv_sum[:, :, :],
                                    conv_hi[:, :, BLOCKS, :].bitcast(F32), ALU.subtract)\
                .then_inc(conv_sum_lo_ready, 1)
            pool.wait_ge(map_in, 16)
            nc.gpsimd.tensor_copy(map_f[:, :], map_i[:, :]).then_inc(map_ready, 1)
            pool.wait_ge(map_ready, 1)
            for e in range(E):
                nc.gpsimd.tensor_scalar(is_expert[:, e, :], map_f[:, :], float(e), None,
                                        ALU.is_equal).then_inc(map_ready, 1)
            split_wide(pool, nc.gpsimd, range(1))
            pool.dma_start(biases_sb[:, :], biases.partition_broadcast(P)).then_inc(biases_in, 16)

            def bias_rows(t, k):
                pool.wait_ge(xr_loaded[k], (t - k) * 4 + 16)
                nc.gpsimd.tensor_tensor(xr[k][:, :], xr[k][:, :], base_b_sb[:, :], ALU.add)\
                    .then_inc(xr_biased, 1)

            def terms_low(q, i):
                pool.wait_ge(terms_hi_ready, (q - START + 1) * HALVES)
                nc.gpsimd.tensor_tensor(terms_lo[i][:, :, :, :, :], terms[i][:, :, :, :, :],
                                        terms_hi[i][:, :, :, :, :].bitcast(F32), ALU.subtract)\
                    .then_inc(terms_lo_ready, 1)

            def y_low(t, k):
                pool.wait_ge(y_hi_ready, t + 1)
                nc.gpsimd.tensor_tensor(y_lo[k % 2][:, :, :], y[k % 2][:, :, :],
                                        y_hi[k % 2][:, :, :].bitcast(F32), ALU.subtract)\
                    .then_inc(y_lo_ready, 1)

            y_low(0, 0)

            def step(t, k, p):
                if isinstance(t, int) and t == 0:
                    pool.wait_ge(up_hi_ready, 1)
                    nc.gpsimd.tensor_tensor(up_lo[:, :], up_scaled[:, :],
                                            up_hi[:, :].bitcast(F32), ALU.subtract)\
                        .then_inc(up_lo_ready, 1)
                    y_low(1, 1)
                    pool.wait_ge(biases_in, 16)
                    bias_rows(0, 0)
                    terms_low(2, 0)
                elif isinstance(t, int) and t == 1:
                    y_low(t + 1, k + 1)
                    bias_rows(t, k)
                elif isinstance(t, int) and t == 2:
                    bias_rows(t, k)
                    y_low(t + 1, k + 1)
                    terms_low(3, 1)
                elif isinstance(t, int) and t == 3:
                    y_low(t + 1, k + 1)
                    bias_rows(t, k)
                elif k % 2 == 0:
                    if up_to_tile(t, TILES - 6):
                        terms_low(p + 2, k // 2)
                    if up_to_tile(t, TILES - 2):
                        y_low(t + 1, k + 1)
                    if isinstance(t, int) and t == TILES - 2:
                        bias_rows(t, k)
                elif up_to_tile(t, TILES - 2):
                    bias_rows(t - 1, k - 1)
                    y_low(t + 1, k + 1)
                    bias_rows(t, k)

            each_step(pool, step)
            bias_rows(TILES - 1, (TILES - 1) % XRING)

        @block.tensor
        def _(pe):
            def keep_warm(bank, count):
                for n in range(count):
                    nc.tensor.matmul(bank, zeros[:, 0:P], zeros[:, :], start=True, stop=True)

            def conv(sums, i, h, first, last):
                n = 0
                for w, a in ((conv_hi, x_hi), (conv_lo, x_hi), (conv_hi, x_lo)):
                    for b in range(BLOCKS):
                        mm = nc.tensor.matmul(sums, w[:, h, b, :],
                                              a[i][:, h, first:last, b:b + M], start=n == 0,
                                              stop=n == 3 * BLOCKS - 1)
                        n += 1
                return mm

            def conv_half(t, k, p):
                if not from_tile(t, START):
                    pe.wait_ge(y_rows_ready, t + 1)
                    pe.wait_ge(x_lo_first, t + 3)
                    conv(conv_ps[:, k, :, :], 1, k, 0, PAIR).then_inc(conv_done, 1)
                    return
                i, h = (k // 2 + 1) % 2, k % 2
                if not from_tile(t, START + 1):
                    pe.wait_ge(conv_sum_lo_ready, 1)
                pe.wait_ge(y_rows_ready, t + 2)
                pe.wait_ge(terms_lo_ready, p)
                for j in (TERMS - 1, 0, 1):
                    sums = common_ps if j == TERMS - 1 else own_ps[:, j, :, :]
                    for w, a in ((conv_hi, terms_hi), (conv_lo, terms_hi), (conv_hi, terms_lo)):
                        mm = nc.tensor.matmul(sums, w[:, h, j, :], a[i][:, h, j, :, :],
                                              start=w is conv_hi and a is terms_hi,
                                              stop=a is terms_lo)
                    if j == TERMS - 1:
                        mm.then_inc(common_done, 1)
                mm.then_inc(conv_done, 1)

            def turn(t, k):
                i = (k // 2) % 2
                if from_tile(t, 1):
                    pe.wait_ge(y_rows_ready, t + 2 - k % 2)
                    pe.wait_ge(y_even_ready, 2 * t)
                    pe.wait_ge(y_odd_ready, 2 * t)
                else:
                    pe.wait_ge(y_rows_first, HALVES)
                for a in range(Q // 2):
                    for h in range(HALVES):
                        first = Q * (k % 2) + 2 * a
                        mm = nc.tensor.transpose(
                            turn_ps[:, a, h, :, :].rearrange("p r o -> p (r o)"),
                            y_rows[i][:, h, first:first + 2, :].rearrange("p n m -> p (n m)"),
                            ident[:, :])
                mm.then_inc(turned, 1)

            FRONT_BANK, NEXT_BANK = 0, 1
            HIGH, W_REST, Y_REST = (y_hi, wide_hi), (y_hi, wide_lo), (y_lo, wide_hi)

            def linear(t, k, runs, banks=(FRONT_BANK, NEXT_BANK),
                       products=(HIGH, W_REST, Y_REST), last=(RUNS - 1, Y_REST)):
                for r in runs:
                    for product in products:
                        a, w = product
                        for b in banks:
                            columns = (0, FRONT + HALF) if b == FRONT_BANK else (FRONT + HALF, WIDE)
                            mm = nc.tensor.matmul(
                                sums_of(t, k)[:, b, 0:columns[1] - columns[0]], a[k % 2][:, r, :],
                                w[:, r, columns[0]:columns[1]],
                                start=r == 0 and product is HIGH,
                                stop=r == last[0] and product is last[1])
                return mm

            def turn_hw(t, k):
                if from_tile(t, 1):
                    pe.wait_ge(hw_lo_ready, t)
                pe.wait_ge(hw_ready, t + 1)
                nc.tensor.transpose(hwt_ps[:, 0:P], hw[k % 2][:, :], ident[:, :])\
                    .then_inc(hwt_done, 1)

            def up(t, k, groups=((FRONT_BANK, NEXT_BANK),)):
                if not from_tile(t, 1):
                    pe.wait_ge(up_lo_ready, 1)
                pe.wait_ge(hw_hi_ready, t + 1)
                for n, group in enumerate(groups):
                    for a, w in ((hw_hi, up_hi), (hw_hi, up_lo), (hw_lo, up_hi)):
                        if a is hw_lo and n == 0:
                            pe.wait_ge(hw_lo_ready, t + 1)
                        for b in group:
                            first = FRONT if b == FRONT_BANK else 0
                            mm = nc.tensor.matmul(
                                sums_of(t, k)[:, b, first:first + HALF], a[k % 2][:, :],
                                w[:, b * HALF:(b + 1) * HALF], start=False, stop=True,
                                skip_group_check=True)
                    mm.then_inc(out_done, 1)

            pe.wait_ge(zeros_ready, 1)
            keep_warm(wide_ps[1][:, 1, :], WARM_UP)
            pe.wait_ge(cond_in, 16)
            for h in range(HALVES):
                mm = nc.tensor.matmul(cond_ps[:, h, :], cond_w_sb[:, h, :], cond_t_sb[:, :],
                                      start=True, stop=True)
            mm.then_inc(cond_summed, 1)
            for a in range(PAIR // Q):
                pe.wait_ge(x_lo_first, a + 1)
                for h in range(HALVES):
                    if a == 0:
                        pe.wait_ge(conv_lo_ready, h + 1)
                    sums = first_ps[:, h, :, :] if a == 0 else conv_ps[:, h, Q:, :]
                    mm = conv(sums, 0, h, a * Q, (a + 1) * Q)
                mm.then_inc(conv_done, 1)
            pe.wait_ge(ident_ready, 1)
            turn(0, 0)
            keep_warm(wide_ps[1][:, 1, :], WARM_BETWEEN)

            def first_step():
                runs = range(RUNS)
                pe.wait_ge(y_hi_ready, 1)
                for r in runs:
                    if r == RUNS - 1:
                        turn(1, 1)
                    pe.wait_ge(wide_hi_ready, r + 1)
                    linear(0, 0, (r,), products=(HIGH,))
                pe.wait_ge(y_lo_ready, 1)
                linear(0, 0, runs, products=(Y_REST,), last=(RUNS - 1, W_REST))
                pe.wait_ge(wide_lo_ready, RUNS)
                for bank, done in ((FRONT_BANK, front_done), (NEXT_BANK, linear_done)):
                    linear(0, 0, runs, (bank,), (W_REST,), (RUNS - 1, W_REST)).then_inc(done, 1)
                conv_half(0, 0, 0)

            def step(t, k, p):
                runs = range(RUNS)
                if isinstance(t, int) and t == 0:
                    return first_step()
                if isinstance(t, int) and t == TILES:
                    keep_warm(turn_ps[:, :, :, :, :].rearrange("p a h r o -> p (a h r o)"),
                              WARM_END)
                    turn_hw(t - 1, k - 1)
                    return up(t - 1, k - 1, ((FRONT_BANK,), (NEXT_BANK,)))
                if up_to_tile(t, TILES - 3):
                    conv_half(t, k, p)
                elif t == TILES - 2:
                    turn(t + 1, k + 1)
                if from_tile(t, 2) and up_to_tile(t, TILES - 3):
                    pe.wait_ge(out_added, t - 1)
                elif not up_to_tile(t, TILES - 2):
                    pe.wait_ge(out_added, t - 2)
                pe.wait_ge(y_lo_ready, t + 1)
                linear(t, k, runs[:2], (FRONT_BANK,))
                linear(t, k, runs[2:3], (FRONT_BANK,), (HIGH,))
                if up_to_tile(t, TILES - 3):
                    turn(t + 1, k + 1)
                linear(t, k, runs[2:3], (FRONT_BANK,), (W_REST, Y_REST))
                linear(t, k, runs[3:], (FRONT_BANK,)).then_inc(front_done, 1)
                turn_hw(t - 1, k - 1)
                linear(t, k, runs[:3], (NEXT_BANK,))
                up(t - 1, k - 1)
                linear(t, k, runs[3:], (NEXT_BANK,)).then_inc(linear_done, 1)

            each_step(pe, step)

        @block.vector
        def _(dve):
            def x_low_first(i, part):
                nc.vector.tensor_tensor(x_lo[i][part], x_in[i][part], x_hi[i][part].bitcast(F32),
                                        ALU.subtract).then_inc(x_lo_first, 1)

            def add_out(t, k):
                dve.wait_ge(xr_biased, t + 1)
                dve.wait_ge(out_done, t + 1)
                rows = xr[k][:, :].rearrange("p (b n) -> p b n", b=2)
                nc.vector.tensor_tensor(rows, linear_sums(t, k), rows, ALU.add)\
                    .then_inc(out_added, 1)

            def add_condition(rows, sums, c, ready):
                batches = c.shape[1]
                nc.vector.tensor_tensor(
                    rows.rearrange("p n (a k) -> p n k a", a=2),
                    sums.rearrange("p n (k a) -> p n k a", a=2),
                    c.unsqueeze(2).unsqueeze(3).to_broadcast([P, batches, MK, 2]), ALU.add)\
                    .then_inc(ready, 1)

            def condition_common(t, k, p):
                dve.wait_ge(common_done, t - 1)
                if from_tile(t, START + 1):
                    dve.wait_ge(y_rows_ready, t + 2)
                c = cond_sb[:, k % 2, bass.ds((p + 1) * PAIR, PAIR)]
                nc.vector.tensor_tensor(common[:, :, :], common_ps,
                                        c.unsqueeze(2).to_broadcast([P, PAIR, MK]), ALU.add)\
                    .then_inc(common_ready, 1)

            def condition(t, k, p):
                i, h = (k // 2 + 1) % 2, k % 2
                if from_tile(t, 2):
                    dve.wait_ge(turned, t - k % 2)
                dve.wait_ge(conv_done, t + 3)
                if not from_tile(t, START):
                    c = cond_sb[:, h, (p + 1) * PAIR:(p + 2) * PAIR]
                    add_condition(y_rows[i][:, h, :, :], conv_ps[:, h, :, :], c, y_rows_ready)
                    return
                dve.wait_ge(common_ready, t - 1)
                nc.vector.tensor_tensor(
                    y_rows[i][:, h, :, :].rearrange("p n (a k) -> p a n k", a=2), own_ps,
                    common[:, :, :].unsqueeze(1).to_broadcast([P, 2, PAIR, MK]), ALU.add)\
                    .then_inc(y_rows_ready, 1)

            def difference(q, i, j):
                dve.wait_ge(terms_loaded[i], (q - i) * 16)
                nc.vector.tensor_tensor(terms[i][:, :, j, :, :], even[i][:, :, :, j:j + MK],
                                        terms[i][:, :, TERMS - 1, :, :], ALU.subtract)\
                    .then_inc(differences_ready, 1)

            def choose(t, k):
                i = k % 2
                dve.wait_ge(front_done, t + 1)
                nc.vector.tensor_tensor(logits[i][:, :], sums_of(t, k)[:, 0, HR:HR + ROUTES],
                                        router_b_sb[:, :], ALU.add).then_inc(logits_ready, 1)
                dve.wait_ge(logits_ready, t + 1)
                nc.vector.tensor_reduce(best[i][:, :], logits[i][:, :], AX_X, ALU.max)\
                    .then_inc(best_ready, 1)
                nc.vector.max(top[i][:, :], logits[i][:, :]).then_inc(top_ready, 1)

            def shift(t, k):
                i = k % 2
                dve.wait_ge(top_ready, t + 1)
                dve.wait_ge(best_ready, t + 1)
                nc.vector.tensor_scalar(shifted[i][:, :], logits[i][:, :], best[i][:, 0:1], None,
                                        ALU.subtract).then_inc(shifted_ready, 1)

            def mark(t, k):
                i = k % 2
                nc.vector.match_replace(rest[i][:, :], top[i][:, :], logits[i][:, :], LOWEST)\
                    .then_inc(rest_ready, 1)
                dve.wait_ge(rest_ready, t + 1)
                nc.vector.tensor_tensor(chosen[i][:, :], rest[i][:, :], logits[i][:, :],
                                        ALU.not_equal).then_inc(chosen_ready, 1)

            def invert(t, k):
                dve.wait_ge(exps_ready, t + 1)
                nc.vector.reciprocal(inv[k % 2][:, :], total[k % 2][:, :]).then_inc(inv_ready, 1)

            def weigh_routes(t, k):
                i = k % 2
                dve.wait_ge(chosen_ready, t + 1)
                dve.wait_ge(inv_ready, t + 1)
                nc.vector.scalar_tensor_tensor(out=weight[i][:, :], in0=exps[i][:, :],
                                               scalar=inv[i][:, 0:1], in1=chosen[i][:, :],
                                               op0=ALU.mult, op1=ALU.mult).then_inc(weight_ready, 1)

            def weigh_experts(t, k):
                i = k % 2
                dve.wait_ge(weight_ready, t + 1)
                nc.vector.tensor_tensor(spread[i][:, :, :], is_expert[:, :, :],
                                        weight[i][:, :].unsqueeze(1).to_broadcast([P, E, ROUTES]),
                                        ALU.mult).then_inc(spread_ready, 1)
                dve.wait_ge(spread_ready, t + 1)
                nc.vector.tensor_reduce(expert_w[i][:, :], spread[i][:, :, :], AX_X, ALU.add)\
                    .then_inc(expert_w_ready, 1)
                if from_tile(t, 2):
                    dve.wait_ge(hwt_done, t - 1)
                dve.wait_ge(expert_w_ready, t + 1)
                nc.vector.tensor_tensor(
                    hw[i][:, :].rearrange("p (e r) -> p e r", e=E),
                    sums_of(t, k)[:, 0, 0:HR].rearrange("p (e r) -> p e r", e=E),
                    expert_w[i][:, :].unsqueeze(2).to_broadcast([P, E, R]),
                    ALU.mult).then_inc(hw_ready, 1)

            def y_even(t, k):
                if from_tile(t, 2):
                    dve.wait_ge(y_lo_ready, t - 1)
                dve.wait_ge(turned, t + 1)
                copy_turned(nc.vector.tensor_copy, t, k, 0, y_even_ready)

            def hw_low(t, k):
                dve.wait_ge(hw_hi_ready, t + 1)
                if from_tile(t, 2):
                    dve.wait_ge(out_done, t - 1)
                nc.vector.tensor_tensor(hw_lo[k % 2][:, :], hwt_ps[:, 0:P],
                                        hw_hi[k % 2][:, :].bitcast(F32), ALU.subtract)\
                    .then_inc(hw_lo_ready, 1)

            every = slice(None)
            dve.wait_ge(x_first_in, 16)
            nc.vector.tensor_copy(x_hi[0][:, :, 0:Q, :], x_in[0][:, :, 0:Q, :])\
                .then_inc(x_hi_first, 1)
            dve.wait_ge(x_hi_first, 1)
            x_low_first(0, (every, every, slice(0, Q), every))
            for h in range(HALVES):
                dve.wait_ge(conv_hi_ready, h + 1)
                nc.vector.tensor_tensor(conv_lo[:, h, 0:BLOCKS, :], conv_sb[:, h, :, :],
                                        conv_hi[:, h, 0:BLOCKS, :].bitcast(F32), ALU.subtract)\
                    .then_inc(conv_lo_ready, 1)
            dve.wait_ge(x_hi_ready, 1)
            x_low_first(0, (every, every, slice(Q, PAIR), every))
            dve.wait_ge(cond_summed, 1)
            for h in range(HALVES):
                nc.vector.tensor_scalar(cond_sb[:, h, :], cond_ps[:, h, :], conv_b_sb[:, h:h + 1],
                                        None, ALU.add).then_inc(cond_biased, 1)
            dve.wait_ge(cond_biased, HALVES)
            for a, sums, ready in ((0, first_ps, y_rows_first),
                                   (1, conv_ps[:, :, Q:, :], y_rows_ready)):
                dve.wait_ge(conv_done, a + 1)
                own = slice(a * Q, (a + 1) * Q)
                for h in range(HALVES):
                    add_condition(y_rows[0][:, h, own, :], sums[:, h, :, :], cond_sb[:, h, own],
                                  ready)
                if a == 0:
                    y_even(0, 0)
            split_wide(dve, nc.vector, range(1, RUNS))
            dve.wait_ge(x_hi_ready, 2)
            for h in range(HALVES):
                x_low_first(1, (every, h, every, every))

            def step(t, k, p):
                if isinstance(t, int) and t == 0:
                    y_even(1, 1)
                    for j in range(2):
                        difference(2, 0, j)
                    condition(t, k, p)
                    dve.wait_ge(biases_in, 16)
                    choose(t, k)
                    shift(t, k)
                    mark(t, k)
                    return
                if isinstance(t, int) and t >= TILES - 2:
                    return last_steps(t, k)
                if from_tile(t, START):
                    condition_common(t, k, p)
                    invert(t - 1, k - 1)
                    condition(t, k, p)
                    weigh_routes(t - 1, k - 1)
                else:
                    condition(t, k, p)
                    invert(t - 1, k - 1)
                    weigh_routes(t - 1, k - 1)
                    dve.wait_ge(map_ready, 1 + E)
                weigh_experts(t - 1, k - 1)
                y_even(t + 1, k + 1)
                if from_tile(t, 2):
                    if up_to_tile(t, TILES - 7):
                        difference(p + 3, (k // 2 + 1) % 2, k % 2)
                    hw_low(t - 1, k - 1)
                else:
                    hw_low(t - 1, k - 1)
                    difference(3, 1, 0)
                choose(t, k)
                shift(t, k)
                mark(t, k)
                add_out(t - 1, (k - 1) % UNROLL)
                if not from_tile(t, 2):
                    difference(3, 1, 1)

            def last_steps(t, k):
                if t == TILES - 2:
                    y_even(t + 1, k + 1)
                invert(t - 1, k - 1)
                weigh_routes(t - 1, k - 1)
                weigh_experts(t - 1, k - 1)
                if t == TILES - 2:
                    hw_low(t - 1, k - 1)
                    choose(t, k)
                    shift(t, k)
                    mark(t, k)
                elif t == TILES - 1:
                    add_out(t - 2, (k - 2) % UNROLL)
                    choose(t, k)
                    shift(t, k)
                    hw_low(t - 1, k - 1)
                    mark(t, k)
                else:
                    add_out(t - 2, (k - 2) % UNROLL)
                    hw_low(t - 1, k - 1)

            each_step(dve, step)
            dve.wait_ge(xr_biased, TILES)
            for b in range(2):
                half = xr[(TILES - 1) % XRING][:, b * HALF:(b + 1) * HALF]
                dve.wait_ge(out_done, TILES + b)
                nc.vector.tensor_tensor(half, linear_sums(TILES - 1, 1)[:, b, :], half, ALU.add)\
                    .then_inc(out_added, 1)


def kernel(x, cond_128, fside_S_0, L0_cond_weight, L0_cond_c_weight, L0_ffn_base_W, L0_ffn_base_b,
           L0_ffn_router_W, L0_ffn_router_b, L0_ffn_A, L0_ffn_B, L0_ffn_expert_map):
    import numpy as np
    from concourse import bacc
    from concourse.bass_utils import run_bass_kernel_spmd

    def in_turn_order(a):
        return np.asarray(a).reshape(TILES, 2, Q // 2, -1).transpose(0, 2, 1, 3).reshape(a.shape)

    x = np.asarray(x)
    per = C // GROUPS
    blocks = np.pad(in_turn_order(x), ((0, 0), (0, 0), (PAD, BP - PAD)))
    blocks = blocks.reshape(N // PAIR, PAIR, HALVES, CH, MI, BP).transpose(0, 5, 3, 2, 1, 4)
    blocks = blocks.reshape(N // PAIR, P, HALVES, PAIR, MI)

    w = np.asarray(L0_cond_weight)
    conv = np.zeros((BP, CH, HALVES, BLOCKS, BP, CH), w.dtype)
    for b in range(BLOCKS):
        for s in range(BP):
            for r in range(BP):
                tap = BP * b + s - r
                if 0 <= tap < TAPS:
                    for g in range(GROUPS):
                        h, own = g * per // CH, slice(g * per % CH, g * per % CH + per)
                        conv[s, own, h, b, r, own] = w[g * per:(g + 1) * per, :, tap].T

    def by_output_row(a):
        a = np.asarray(a).reshape(HALVES, CH, -1)
        return np.stack([a] * BP).transpose(0, 2, 1, 3).reshape(P, HALVES, -1)

    def by_position(a):
        a = np.asarray(a).reshape(-1, MK, 2, 2, RUNS)
        return a.transpose(3, 2, 1, 4, 0).reshape(P, RUNS, -1)

    columns = [by_position(L0_ffn_A), by_position(L0_ffn_router_W), by_position(L0_ffn_base_W)]
    columns[1] = np.pad(columns[1], ((0, 0), (0, 0), (0, FRONT - HR - ROUTES)))
    given = {
        "x_start": blocks[:START],
        "x_even": blocks[START:, ..., 0::2],
        "x_odd": blocks[START:, ..., 1::2],
        "x_rows": x.reshape(TILES, P, L),
        "conv_w": conv.reshape(P, HALVES, BLOCKS, P),
        "cond": np.concatenate([in_turn_order(cond_128).T,
                                by_output_row(L0_cond_c_weight).transpose(2, 1, 0).reshape(P, -1),
                                by_output_row(fside_S_0).reshape(P, HALVES)], axis=1),
        "wide_w": np.concatenate(columns, axis=2),
        "up_w": np.asarray(L0_ffn_B).transpose(0, 2, 1).reshape(E * R, L),
        "biases": np.concatenate([L0_ffn_base_b, L0_ffn_router_b]),
        "expert_map": L0_ffn_expert_map,
    }
    nc = bacc.Bacc("TRN2", target_bir_lowering=False, num_devices=1)
    arrays, args = {}, []
    for name, a in given.items():
        a = np.ascontiguousarray(a)
        arrays[name] = a
        args.append(nc.dram_tensor(name, a.shape, mybir.dt.from_np(a.dtype),
                                   kind="ExternalInput").ap())
    out = nc.dram_tensor("out", (TILES, P, L), F32, kind="ExternalOutput").ap()
    build(nc, *args, out)
    r = run_bass_kernel_spmd(nc, [arrays], core_ids=[0])
    return r.results[0]["out"].reshape(N, C, L)
```
